# Optimizing a Trainium2 kernel written in Bass

```python
import numpy as np
import jax
import jax.numpy as jnp

def _softmax(x, axis=-1):
    return jax.nn.softmax(x, axis=axis)
def _gelu(x):
    return jax.nn.gelu(x, approximate=True)
def _silu(x):
    return jax.nn.silu(x)
def _sigmoid(x):
    return jax.nn.sigmoid(x)
def _layernorm(x, axis=-1, eps=1e-5):
    m = jnp.mean(x, axis=axis, keepdims=True)
    v = jnp.var(x, axis=axis, keepdims=True)
    return (x - m) / jnp.sqrt(v + eps)
def _scatter_add(tgt, idx, src, axis=0):
    return tgt.at[idx].add(src)
def _segment_sum(src, seg, n):
    return jax.ops.segment_sum(src, seg, n)

kernel_name = 'mk_conv_seq_d1_conv_nchw512_364b45'

def setup_inputs(seed: int = 0):
    np.random.seed(seed)
    _w = jnp.asarray
    def _rec_inputs():
        import jax
        import jax.numpy as jnp
        _gk = jax.random.key(seed)
        x = 7.22e-05 + 1 * jax.random.normal(jax.random.fold_in(_gk, 1), (16, 512, 32, 32), jnp.float32)
        return x
    x = _rec_inputs()
    def _L0_conv_setup():
        import jax, jax.numpy as jnp
        import numpy as np
        NUM_GROUPS = 32
        EPS = 1e-06

        def group_norm(x, gamma, beta):
            B, C, H, W = x.shape
            xg = x.reshape(B, NUM_GROUPS, C // NUM_GROUPS, H, W)
            mean = jnp.mean(xg, axis=(2, 3, 4), keepdims=True)
            var = jnp.var(xg, axis=(2, 3, 4), keepdims=True)
            xn = ((xg - mean) * jax.lax.rsqrt(var + EPS)).reshape(B, C, H, W)
            return xn * gamma[None, :, None, None] + beta[None, :, None, None]

        def conv1x1(x, w, b):
            return jnp.einsum('oc,bchw->bohw', w, x) + b[None, :, None, None]
        key = jax.random.key(seed)
        ks = jax.random.split(key, 10)
        B, C, H, W = (16, 512, 32, 32)
        s = 1.0 / np.sqrt(C)
        inp = {'hidden_states': jax.random.normal(ks[0], (B, C, H, W), dtype=jnp.float32), 'norm_gamma': jnp.ones((C,), dtype=jnp.float32), 'norm_beta': jnp.zeros((C,), dtype=jnp.float32), 'wq': jax.random.normal(ks[1], (C, C), dtype=jnp.float32) * s, 'bq': jnp.zeros((C,), dtype=jnp.float32), 'wk': jax.random.normal(ks[2], (C, C), dtype=jnp.float32) * s, 'bk': jnp.zeros((C,), dtype=jnp.float32), 'wv': jax.random.normal(ks[3], (C, C), dtype=jnp.float32) * s, 'bv': jnp.zeros((C,), dtype=jnp.float32), 'wo': jax.random.normal(ks[4], (C, C), dtype=jnp.float32) * s, 'bo': jnp.zeros((C,), dtype=jnp.float32)}
        return inp
    _L0_conv_all = _L0_conv_setup()
    _L0_conv_in = {k: v for k, v in _L0_conv_all.items() if k in ('norm_gamma', 'norm_beta', 'wq', 'bq', 'wk', 'bk', 'wv', 'bv', 'wo', 'bo', )}
    del _L0_conv_all

    return {
        "x": x,
        "L0_conv_norm_gamma": _L0_conv_in["norm_gamma"],
        "L0_conv_norm_beta": _L0_conv_in["norm_beta"],
        "L0_conv_wq": _L0_conv_in["wq"],
        "L0_conv_bq": _L0_conv_in["bq"],
        "L0_conv_wk": _L0_conv_in["wk"],
        "L0_conv_bk": _L0_conv_in["bk"],
        "L0_conv_wv": _L0_conv_in["wv"],
        "L0_conv_bv": _L0_conv_in["bv"],
        "L0_conv_wo": _L0_conv_in["wo"],
        "L0_conv_bo": _L0_conv_in["bo"],
    }

def reference(x, L0_conv_norm_gamma, L0_conv_norm_beta, L0_conv_wq, L0_conv_bq, L0_conv_wk, L0_conv_bk, L0_conv_wv, L0_conv_bv, L0_conv_wo, L0_conv_bo):
    import jax
    import jax.numpy as jnp
    def _L0_conv_ref(hidden_states, norm_gamma, norm_beta, wq, bq, wk, bk, wv, bv, wo, bo):
        import jax, jax.numpy as jnp
        import numpy as np
        NUM_GROUPS = 32
        EPS = 1e-06

        def group_norm(x, gamma, beta):
            B, C, H, W = x.shape
            xg = x.reshape(B, NUM_GROUPS, C // NUM_GROUPS, H, W)
            mean = jnp.mean(xg, axis=(2, 3, 4), keepdims=True)
            var = jnp.var(xg, axis=(2, 3, 4), keepdims=True)
            xn = ((xg - mean) * jax.lax.rsqrt(var + EPS)).reshape(B, C, H, W)
            return xn * gamma[None, :, None, None] + beta[None, :, None, None]

        def conv1x1(x, w, b):
            return jnp.einsum('oc,bchw->bohw', w, x) + b[None, :, None, None]
        residual = hidden_states
        h = group_norm(hidden_states, norm_gamma, norm_beta)
        q = conv1x1(h, wq, bq)
        k = conv1x1(h, wk, bk)
        v = conv1x1(h, wv, bv)
        B, C, H, W = q.shape
        N = H * W
        qf = q.reshape(B, C, N)
        kf = k.reshape(B, C, N)
        vf = v.reshape(B, C, N)
        scale = float(C) ** (-0.5)
        attn = jnp.einsum('bci,bcj->bij', qf, kf) * scale
        attn = jax.nn.softmax(attn, axis=2)
        out = jnp.einsum('bcj,bij->bci', vf, attn).reshape(B, C, H, W)
        out = conv1x1(out, wo, bo)
        return residual + out

    def _gn(v, G=32, eps=1e-5):
        B_, C_, H_, W_ = v.shape
        g = v.reshape(B_, G, C_ // G, H_, W_)
        m = jnp.mean(g, axis=(2, 3, 4), keepdims=True)
        s = jnp.var(g, axis=(2, 3, 4), keepdims=True)
        return ((g - m) / jnp.sqrt(s + eps)).reshape(v.shape)

    def _ln_c(v, eps=1e-6):
        m = jnp.mean(v, axis=1, keepdims=True)
        s = jnp.var(v, axis=1, keepdims=True)
        return (v - m) / jnp.sqrt(s + eps)

    def _ln_t(v, eps=1e-5):
        m = jnp.mean(v, axis=-1, keepdims=True)
        s = jnp.var(v, axis=-1, keepdims=True)
        return (v - m) / jnp.sqrt(s + eps)

    def _to_tokens(v):
        B_, C_, H_, W_ = v.shape
        return v.reshape(B_, C_, H_ * W_).transpose(0, 2, 1)
    def _from_tokens(t, like):
        B_, C_, H_, W_ = like.shape
        return t.transpose(0, 2, 1).reshape(B_, C_, H_, W_)

    x = _L0_conv_ref(x, L0_conv_norm_gamma, L0_conv_norm_beta, L0_conv_wq, L0_conv_bq, L0_conv_wk, L0_conv_bk, L0_conv_wv, L0_conv_bv, L0_conv_wo, L0_conv_bo)
    return x


_drawn_inputs = setup_inputs


def setup_inputs(seed=0):
    import zlib

    import numpy as np

    out = dict(_drawn_inputs(seed))
    spreads = {'L0_conv_norm_gamma': (1.0, 0.2),
     'L0_conv_norm_beta': (0.0, 0.1),
     'L0_conv_bq': (0.0, 0.8),
     'L0_conv_bk': (0.0, 0.8),
     'L0_conv_bv': (0.0, 0.1),
     'L0_conv_bo': (0.0, 0.1)}
    factors = {}
    for name, (base, spread) in spreads.items():
        noise = np.random.default_rng([zlib.crc32(name.encode()), seed]).standard_normal(out[name].shape)
        drawn = base * np.exp(spread * noise) if base else spread * noise
        out[name] = jnp.asarray(drawn.astype(out[name].dtype))
    for name, factor in factors.items():
        out[name] = (out[name] * factor).astype(out[name].dtype)
    return out
```

```python
from contextlib import ExitStack

import concourse.bass as bass
from concourse import mybir

F32 = mybir.dt.float32
F32R = mybir.dt.float32r
ALU = mybir.AluOpType
ACT = mybir.ActivationFunctionType
MAX_ALL = bass.bass_isa.ReduceOp.max
ADD_ALL = bass.bass_isa.ReduceOp.add

P = 128
GROUPS = 32
EPS = 1e-6


def attention_program(nc, x, gamma, beta, wq, bq, wk, wv, bv, wo, bo, out):
    B, C, H, W = x.shape
    N = H * W
    KC = C // P
    NJ = N // P
    HALF = N // 2
    CG = C // GROUPS
    SCALE = float(C) ** -0.5
    PIECES = N * KC // HALF
    assert HALF == 512 and C == 512 and NJ == 2 * KC and P % CG == 0 and B % 2 == 0 and B >= 4

    x_d = x.rearrange("b (k p) h w -> b p k (h w)", p=P)
    out_d = out.rearrange("b (k p) h w -> b k p (h w)", p=P)
    w_d = {n: a.rearrange("(k p) n -> p k n", p=P) for n, a in (("q", wq), ("k", wk), ("v", wv), ("o", wo))}
    vec_d = [a.rearrange("(k p) -> p k", p=P) for a in (gamma, beta, bq, bv, bo)]

    with ExitStack() as ctx:
        def sb(name, shape, dt=F32):
            return ctx.enter_context(nc.sbuf_tensor(name, [P, *shape], dt))

        def sem(name):
            return ctx.enter_context(nc.semaphore(name))

        wkq_hi, wkq_lo = sb("wkq_hi", [KC, C], F32R), sb("wkq_lo", [KC, C], F32R)
        wov_hi, wov_lo = sb("wov_hi", [KC, C], F32R), sb("wov_lo", [KC, C], F32R)
        h_hi, h_lo = sb("h_hi", [KC, N], F32R), sb("h_lo", [KC, N], F32R)
        t_hi, t_lo = sb("t_hi", [KC, HALF], F32R), sb("t_lo", [KC, HALF], F32R)
        v_hi, v_lo = sb("v_hi", [NJ, C], F32R), sb("v_lo", [NJ, C], F32R)
        p_hi, p_lo = sb("p_hi", [NJ, HALF], F32R), sb("p_lo", [NJ, HALF], F32R)
        xt = sb("xt", [2, KC, N])
        scores = sb("scores", [NJ, HALF])
        stage = sb("stage", [2, HALF])
        run_max, all_max = sb("run_max", [HALF]), sb("all_max", [HALF])
        run_sum, inv_sum = sb("run_sum", [HALF]), sb("inv_sum", [HALF])
        ident, group_mean = sb("ident", [P]), sb("group_mean", [P])
        vecs = sb("vecs", [5, KC])
        gamma_s, beta_s, bq_s, bv_s, bo_s = (vecs[:, n, :] for n in range(5))
        t_bias, out_bias = sb("t_bias", [KC]), sb("out_bias", [KC])
        bn = sb("bn", [PIECES, 6])
        chan = sb("chan", [KC, 2])
        mean_g, diff, spread = sb("mean_g", [KC]), sb("diff", [KC]), sb("spread", [KC])
        var_g, rstd, minus_half = sb("var_g", [KC]), sb("rstd", [KC]), sb("minus_half", [KC])
        h_scale, h_shift, shift0 = sb("h_scale", [KC]), sb("h_shift", [KC]), sb("shift0", [KC])

        wq_raw, wk_raw, wo_t = scores[:, 0:KC, :], scores[:, KC:2 * KC, :], scores[:, 0:KC, :]
        raw = xt[:, 1, :, :].rearrange("p k n -> p (k n)")
        wv_raw = raw[:, 0:KC * C].rearrange("p (k n) -> p k n", k=KC)
        wo_raw = raw[:, KC * C:2 * KC * C].rearrange("p (k n) -> p k n", k=KC)

        bank = [ctx.enter_context(nc.psum_tensor(f"bank{n}", [P, 512], F32)) for n in range(8)]

        def t_bank(half, c):
            return bank[4 * half + c]

        def v_bank(j):
            return bank[(4 + j) % 8]

        def s_bank(half, j):
            return bank[j if half else (4 + j) % 8]

        def o_bank(half, c):
            return bank[4 * half + c]

        MEAN_BANK, VAR_BANK = bank[3], bank[4]

        wq_in, wk_in, wv_in, wo_in, vec_in = (sem(n) for n in ("wq_in", "wk_in", "wv_in", "wo_in", "vec_in"))
        x_in = [sem("x_in0"), sem("x_in1")]
        out_stored = [sem("out_stored0"), sem("out_stored1")]
        consts_set, max_all, sum_all, rstd_set = (sem(n) for n in ("consts_set", "max_all", "sum_all", "rstd_set"))
        reduce_begun = sem("reduce_begun")
        wkq_summed, wov_summed, bias_summed, wo_turned = (
            sem(n) for n in ("wkq_summed", "wov_summed", "bias_summed", "wo_turned"))
        t_summed, v_summed, s_summed, o_summed = (sem(n) for n in ("t_summed", "v_summed", "s_summed", "o_summed"))
        mean_summed, var_summed, p_used = (sem(n) for n in ("mean_summed", "var_summed", "p_used"))
        w_high, wo_t_set, t_high, v_high, h_high, p_high, s_copied, exp_set = (
            sem(n) for n in ("w_high", "wo_t_set", "t_high", "v_high", "h_high", "p_high", "s_copied", "exp_set"))
        w_split, biases_set, t_split, v_split, h_split, p_split = (
            sem(n) for n in ("w_split", "biases_set", "t_split", "v_split", "h_split", "p_split"))
        max_step, centred, sum_step, inv_set = (sem(n) for n in ("max_step", "centred", "sum_step", "inv_set"))
        bn_set, chan_set, mean_step, spread_set, var_set, scale_step, h_full = (
            sem(n) for n in ("bn_set", "chan_set", "mean_step", "spread_set", "var_set", "scale_step", "h_full"))
        o_scaled, o_done = sem("o_scaled"), sem("o_done")

        block = ctx.enter_context(nc.Block())

        def images(engine, batch):
            with engine.Fori(0, B - 2, 2) as b:
                batch(b, 0, True)
                batch(b + 1, 1, True)
            batch(B - 2, 0, True)
            batch(B - 1, 1, False)

        def count(b, per_image, step):
            return b * per_image + step

        @block.sync
        def _(sp):
            sp.dma_start(wk_raw, w_d["k"]).then_inc(wk_in, 16)
            sp.dma_start(wq_raw, w_d["q"]).then_inc(wq_in, 16)
            sp.dma_start(xt[:, 0, :, :], x_d[0]).then_inc(x_in[0], 16)
            sp.dma_start(wo_raw, w_d["o"]).then_inc(wo_in, 16)
            sp.dma_start(wv_raw, w_d["v"]).then_inc(wv_in, 16)
            for s in range(2):
                sp.sem_inc(out_stored[s], 16)

            def batch(b, par, more):
                if more:
                    sp.wait_ge(o_done, count(b, 8, 8))
                    sp.dma_start(xt[:, 1 - par, :, :], x_d[b + 1]).then_inc(x_in[1 - par], 16)
                for n in range(2 * KC):
                    half, c = divmod(n, KC)
                    sp.wait_ge(o_done, count(b, 8, 8 + n + 1))
                    sp.dma_start(out_d[b, c, :, half * HALF:(half + 1) * HALF],
                                 stage[:, n % 2, :]).then_inc(out_stored[n % 2], 16)

            images(sp, batch)
            for s in range(2):
                sp.wait_ge(out_stored[s], 16 * (1 + B * KC))

        @block.gpsimd
        def _(pool):
            for n, a in enumerate(vec_d):
                pool.dma_start(vecs[:, n, :], a, allow_slow_non_contiguous=True).then_inc(vec_in, 16)
            nc.gpsimd.memset(ident[:], 0.0).then_inc(consts_set, 1)
            nc.gpsimd.memset(group_mean[:], 1.0 / CG).then_inc(consts_set, 1)
            nc.gpsimd.memset(minus_half[:], -0.5).then_inc(consts_set, 1)
            pool.wait_ge(consts_set, 3)
            nc.gpsimd.affine_select(out=ident[:], in_=ident[:], compare_op=ALU.not_equal, fill=1.0, base=0,
                                    pattern=[[-1, P]], channel_multiplier=1).then_inc(consts_set, 1)
            blocks = group_mean[:].rearrange("p (g d) -> p g d", d=CG)
            nc.gpsimd.affine_select(out=blocks, in_=blocks, compare_op=ALU.is_ge, fill=0.0, base=0,
                                    pattern=[[-CG, P // CG], [0, CG]], channel_multiplier=1).then_inc(consts_set, 1)
            pool.wait_ge(consts_set, 5)
            nc.gpsimd.affine_select(out=blocks, in_=blocks, compare_op=ALU.is_ge, fill=0.0, base=CG - 1,
                                    pattern=[[CG, P // CG], [0, CG]], channel_multiplier=-1).then_inc(consts_set, 1)

            def deviation(b):
                pool.wait_ge(var_set, count(b, 1, 1))
                nc.gpsimd.tensor_tensor(rstd[:], var_g[:], minus_half[:], ALU.pow).then_inc(rstd_set, 1)

            deviation(0)

            def batch(b, par, more):
                for half in range(2):
                    pool.wait_ge(max_step, count(b, 2 * (NJ - 1), (half + 1) * (NJ - 1)))
                    pool.sem_inc(reduce_begun, 1)
                    nc.gpsimd.partition_all_reduce(all_max[:], run_max[:], P, MAX_ALL).then_inc(max_all, 1)
                    if half and more:
                        deviation(b + 1)
                    pool.wait_ge(sum_step, count(b, 2 * (NJ - 1), (half + 1) * (NJ - 1)))
                    pool.wait_ge(o_scaled, count(b, 8, 8 + half * KC))
                    pool.sem_inc(reduce_begun, 1)
                    nc.gpsimd.partition_all_reduce(inv_sum[:], run_sum[:], P, ADD_ALL).then_inc(sum_all, 1)

            images(pool, batch)

        @block.tensor
        def _(pe):
            def product(o, a_hi, a_lo, b_hi, b_lo, start, stop):
                nc.tensor.matmul(o, a_hi, b_hi, start=start, stop=False)
                nc.tensor.matmul(o, a_hi, b_lo, start=False, stop=False)
                return nc.tensor.matmul(o, a_lo, b_hi, start=False, stop=stop)

            def cols(n):
                return slice(n * P, (n + 1) * P)

            def group_means(bk, values):
                return nc.tensor.matmul(bk[:, 0:KC], group_mean[:], values, start=True, stop=True)

            pe.wait_ge(wq_in, 16)
            pe.wait_ge(wk_in, 16)
            for c in range(KC):
                for o in range(KC):
                    mm = nc.tensor.matmul(bank[c][:], wq_raw[:, o, cols(c)], wk_raw[:, o, :],
                                          start=(o == 0), stop=(o == KC - 1))
                mm.then_inc(wkq_summed, 1)
            pe.wait_ge(vec_in, 16 * len(vec_d))
            pe.wait_ge(consts_set, 6)
            for c in range(KC):
                for o in range(KC):
                    mm = nc.tensor.matmul(bank[4][:, c:c + 1], wk_raw[:, o, cols(c)], bq_s[:, o:o + 1],
                                          start=(o == 0), stop=(o == KC - 1))
            mm.then_inc(bias_summed, 1)
            pe.wait_ge(chan_set, KC)
            group_means(bank[5], chan[:, :, 0]).then_inc(mean_summed, 1)

            def turn_wo(o):
                for c in range(KC):
                    mm = nc.tensor.transpose(bank[4 + o][:, cols(c)], wo_raw[:, c, cols(o)], ident[:])
                mm.then_inc(wo_turned, 1)

            pe.wait_ge(wo_in, 16)
            pe.wait_ge(biases_set, 1)
            turn_wo(0)
            pe.wait_ge(spread_set, 1)
            group_means(bank[6], spread[:]).then_inc(var_summed, 1)
            turn_wo(1)
            pe.wait_ge(var_set, 1)
            turn_wo(2)
            turn_wo(3)
            pe.wait_ge(wv_in, 16)
            for c in range(KC):
                pe.wait_ge(w_split, c + 1)
                for o in range(KC):
                    pe.wait_ge(wo_t_set, o + 1)
                    mm = nc.tensor.matmul(bank[c][:], wv_raw[:, o, cols(c)], wo_t[:, o, :],
                                          start=(o == 0), stop=(o == KC - 1))
                mm.then_inc(wov_summed, 1)
            for c in range(KC):
                for o in range(KC):
                    mm = nc.tensor.matmul(bank[4][:, c:c + 1], wo_t[:, o, cols(c)], bv_s[:, o:o + 1],
                                          start=(o == 0), stop=(o == KC - 1))
            mm.then_inc(bias_summed, 1)

            def make_t(b, half, more):
                for c in range(KC):
                    if half == 0:
                        pe.wait_ge(o_scaled, count(b, 8, c + 1))
                    else:
                        pe.wait_ge(s_copied, count(b, 16, c + 1))
                    for k in range(KC):
                        if half == 0 and c == 0:
                            pe.wait_ge(h_split, count(b, PIECES, 2 * (k + 1)))
                        q = slice(half * HALF, (half + 1) * HALF)
                        mm = product(t_bank(half, c)[:], wkq_hi[:, k, cols(c)], wkq_lo[:, k, cols(c)],
                                     h_hi[:, k, q], h_lo[:, k, q], k == 0, k == KC - 1)
                    mm.then_inc(t_summed, 1)
                    if half == 1 and more and c == 1:
                        pe.wait_ge(chan_set, count(b, KC, 2 * KC))
                        pe.wait_ge(s_copied, count(b, 16, NJ))
                        group_means(MEAN_BANK, chan[:, :, 0]).then_inc(mean_summed, 1)

            def make_v(b):
                for j in range(NJ):
                    if j < 4:
                        pe.wait_ge(o_scaled, count(b, 8, 4 + j + 1))
                    else:
                        pe.wait_ge(t_split, count(b, 8, j - 4 + 1))
                    for k in range(KC):
                        mm = product(v_bank(j)[:], h_hi[:, k, cols(j)], h_lo[:, k, cols(j)],
                                     wov_hi[:, k, :], wov_lo[:, k, :], k == 0, k == KC - 1)
                    mm.then_inc(v_summed, 1)

            def score(half, j, k):
                return product(s_bank(half, j)[:], h_hi[:, k, cols(j)], h_lo[:, k, cols(j)],
                               t_hi[:, k, :], t_lo[:, k, :], k == 0, k == KC - 1)

            def scores_0(b):
                pe.wait_ge(t_split, count(b, 8, KC))
                for j in range(NJ):
                    pe.wait_ge(v_split, count(b, 8, j + 1))
                    for k in range(KC):
                        mm = score(0, j, k)
                    mm.then_inc(s_summed, 1)

            def scores_1(b, more):
                for k in range(KC):
                    pe.wait_ge(t_split, count(b, 8, KC + k + 1))
                    for j in range(4):
                        if k == 0:
                            pe.wait_ge(s_copied, count(b, 16, j + 4 + 1))
                            if more and s_bank(1, j) is MEAN_BANK:
                                pe.wait_ge(mean_step, count(b, 3, 3 + 1))
                        mm = score(1, j, k)
                        if k == KC - 1:
                            mm.then_inc(s_summed, 1)
                for j in range(4, NJ):
                    for k in range(KC):
                        mm = score(1, j, k)
                    mm.then_inc(s_summed, 1)

            def outputs(b, half, more):
                for j in range(NJ):
                    pe.wait_ge(p_split, count(b, 16, half * NJ + j + 1))
                    for c in range(KC):
                        if j == 0:
                            pe.wait_ge(s_copied, count(b, 16, NJ + 4 * half + c + 1))
                            if more and o_bank(half, c) is VAR_BANK:
                                pe.wait_ge(var_set, count(b, 1, 2))
                        mm = product(o_bank(half, c)[:], v_hi[:, j, cols(c)], v_lo[:, j, cols(c)],
                                     p_hi[:, j, :], p_lo[:, j, :], j == 0, j == NJ - 1)
                        if j == NJ - 1:
                            mm.then_inc(o_summed, 1)
                    if half == 0 and j < NJ - 1:
                        mm.then_inc(p_used, 1)

            def batch(b, par, more):
                make_t(b, 0, more)
                make_v(b)
                scores_0(b)
                make_t(b, 1, more)
                scores_1(b, more)
                if more:
                    pe.wait_ge(spread_set, count(b, 1, 2))
                    pe.wait_ge(s_copied, count(b, 16, NJ + 4 + 1))
                    group_means(VAR_BANK, spread[:]).then_inc(var_summed, 1)
                pe.wait_ge(v_split, count(b, 8, NJ))
                outputs(b, 0, more)
                outputs(b, 1, more)

            images(pe, batch)

        @block.scalar
        def _(act):
            for c in range(KC):
                act.wait_ge(wkq_summed, c + 1)
                nc.scalar.copy(wkq_hi[:, c, :], bank[c][:]).then_inc(w_high, 1)
            for o in range(KC):
                act.wait_ge(wo_turned, o + 1)
                nc.scalar.copy(wo_t[:, o, :], bank[4 + o][:]).then_inc(wo_t_set, 1)
            def high_h(b, par, k):
                act.wait_ge(scale_step, count(b, 3, 3))
                nc.scalar.activation(h_hi[:, k, :], xt[:, par, k, :], ACT.Identity, bias=h_shift[:, k:k + 1],
                                     scale=h_scale[:, k:k + 1]).then_inc(h_high, 1)

            for k in range(KC):
                high_h(0, 0, k)
            for c in range(KC):
                act.wait_ge(wov_summed, c + 1)
                nc.scalar.copy(wov_hi[:, c, :], bank[c][:]).then_inc(w_high, 1)

            def high_t(b, half, c):
                act.wait_ge(t_summed, count(b, 8, half * KC + c + 1))
                nc.scalar.activation(t_hi[:, c, :], t_bank(half, c)[:], ACT.Identity,
                                     bias=t_bias[:, c:c + 1]).then_inc(t_high, 1)

            def copy_scores(b, half, j):
                act.wait_ge(s_summed, count(b, 16, half * NJ + j + 1))
                if half == 0:
                    act.wait_ge(h_split, count(b, PIECES, j + 1))
                else:
                    act.wait_ge(sum_step, count(b, 2 * (NJ - 1), max(j, 1)))
                nc.scalar.copy(scores[:, j, :], s_bank(half, j)[:]).then_inc(s_copied, 1)

            def exponentials(b, half, j):
                act.wait_ge(centred, count(b, 16, half * NJ + j + 1))
                nc.scalar.activation(scores[:, j, :], scores[:, j, :], ACT.Exp, scale=SCALE).then_inc(exp_set, 1)

            def high_p(b, half, j):
                act.wait_ge(exp_set, count(b, 16, half * NJ + j + 1))
                if half == 1 and j < NJ - 1:
                    act.wait_ge(p_used, count(b, NJ - 1, j + 1))
                elif half == 1:
                    act.wait_ge(o_summed, count(b, 8, KC))
                nc.scalar.copy(p_hi[:, j, :], scores[:, j, :]).then_inc(p_high, 1)

            def batch(b, par, more):
                for c in range(KC):
                    high_t(b, 0, c)
                for j in range(NJ):
                    act.wait_ge(v_summed, count(b, 8, j + 1))
                    nc.scalar.copy(v_hi[:, j, :], v_bank(j)[:]).then_inc(v_high, 1)
                for j in range(NJ):
                    copy_scores(b, 0, j)
                high_t(b, 1, 0)
                exponentials(b, 0, 0)
                for j in range(NJ):
                    if j in (1, 3, 4):
                        high_t(b, 1, (1, 3, 4).index(j) + 1)
                    if j + 1 < NJ:
                        exponentials(b, 0, j + 1)
                    high_p(b, 0, j)
                for j in range(NJ):
                    copy_scores(b, 1, j)
                exponentials(b, 1, 0)
                for j in range(NJ):
                    if j + 1 < NJ:
                        exponentials(b, 1, j + 1)
                    high_p(b, 1, j)
                    if more and j < KC:
                        high_h(b + 1, 1 - par, j)

            images(act, batch)

        @block.vector
        def _(dve):
            def piece_of(par, n):
                k, half = divmod(n, 2)
                return k, xt[:, par, k, half * HALF:(half + 1) * HALF]

            def bn_piece(b, par, n):
                k, piece = piece_of(par, n)
                nc.vector.bn_stats(bn[:, n, :], piece).then_inc(bn_set, 1)

            def channel_stats(b):
                for k in range(KC):
                    nc.vector.bn_aggr(chan[:, k, :],
                                       bn[:, 2 * k:2 * k + 2, :].rearrange("p a s -> p (a s)")).then_inc(chan_set, 1)

            def group_spread(b, means=MEAN_BANK):
                dve.wait_ge(mean_summed, count(b, 1, 1))
                nc.vector.tensor_copy(mean_g[:], means[:, 0:KC]).then_inc(mean_step, 1)
                dve.wait_ge(mean_step, count(b, 3, 1))
                dve.wait_ge(chan_set, count(b, KC, KC))
                nc.vector.tensor_tensor(diff[:], chan[:, :, 0], mean_g[:], ALU.subtract).then_inc(mean_step, 1)
                dve.wait_ge(mean_step, count(b, 3, 2))
                nc.vector.tensor_tensor(diff[:], diff[:], diff[:], ALU.mult).then_inc(mean_step, 1)
                dve.wait_ge(mean_step, count(b, 3, 3))
                nc.vector.tensor_tensor(spread[:], diff[:], chan[:, :, 1], ALU.add).then_inc(spread_set, 1)

            def group_variance(b, variances=VAR_BANK):
                dve.wait_ge(var_summed, count(b, 1, 1))
                nc.vector.tensor_scalar(var_g[:], variances[:, 0:KC], EPS, None, ALU.add).then_inc(var_set, 1)

            def affine(b):
                dve.wait_ge(rstd_set, count(b, 1, 1))
                nc.vector.tensor_tensor(h_scale[:], gamma_s, rstd[:], ALU.mult).then_inc(scale_step, 1)
                dve.wait_ge(scale_step, count(b, 3, 1))
                nc.vector.tensor_tensor(shift0[:], mean_g[:], h_scale[:], ALU.mult).then_inc(scale_step, 1)
                dve.wait_ge(scale_step, count(b, 3, 2))
                nc.vector.tensor_tensor(h_shift[:], beta_s, shift0[:], ALU.subtract).then_inc(scale_step, 1)

            def low_h(b, par, n, slot):
                k, piece = piece_of(par, n)
                dve.wait_ge(scale_step, count(b, 3, 3))
                nc.vector.tensor_scalar(scores[:, slot, :], piece, h_scale[:, k:k + 1], h_shift[:, k:k + 1],
                                        ALU.mult, ALU.add).then_inc(h_full, 1)
                q = slice((n % 2) * HALF, (n % 2 + 1) * HALF)
                dve.wait_ge(h_full, count(b, PIECES, n + 1))
                dve.wait_ge(h_high, count(b, KC, k + 1))
                nc.vector.tensor_tensor(h_lo[:, k, q], scores[:, slot, :], h_hi[:, k, q].bitcast(F32),
                                        ALU.subtract).then_inc(h_split, 1)

            dve.wait_ge(x_in[0], 16)
            for n in range(PIECES):
                bn_piece(0, 0, n)
            dve.wait_ge(bn_set, PIECES)
            channel_stats(0)
            for c in range(KC):
                dve.wait_ge(w_high, c + 1)
                nc.vector.tensor_tensor(wkq_lo[:, c, :], bank[c][:], wkq_hi[:, c, :].bitcast(F32),
                                        ALU.subtract).then_inc(w_split, 1)
            dve.wait_ge(bias_summed, 1)
            nc.vector.tensor_copy(t_bias[:], bank[4][:, 0:KC]).then_inc(biases_set, 1)
            group_spread(0, bank[5])
            group_variance(0, bank[6])
            affine(0)
            for n in range(PIECES):
                if n >= KC:
                    dve.wait_ge(h_split, n - KC + 1)
                low_h(0, 0, n, KC + n % KC)
            for c in range(KC):
                dve.wait_ge(w_high, KC + c + 1)
                nc.vector.tensor_tensor(wov_lo[:, c, :], bank[c][:], wov_hi[:, c, :].bitcast(F32),
                                        ALU.subtract).then_inc(w_split, 1)
            dve.wait_ge(bias_summed, 2)
            dve.wait_ge(vec_in, 16 * len(vec_d))
            nc.vector.tensor_tensor(out_bias[:], bank[4][:, 0:KC], bo_s, ALU.add).then_inc(biases_set, 1)
            dve.wait_ge(biases_set, 2)
            dve.sem_inc(o_scaled, 8)
            dve.sem_inc(o_done, 8)

            def low_t(b, half, c):
                dve.wait_ge(t_high, count(b, 8, half * KC + c + 1))
                nc.vector.scalar_tensor_tensor(t_lo[:, c, :], t_bank(half, c)[:], t_bias[:, c:c + 1],
                                               t_hi[:, c, :].bitcast(F32), ALU.add, ALU.subtract).then_inc(t_split, 1)

            def maximum(b, half, j):
                dve.wait_ge(s_copied, count(b, 16, half * NJ + j + 1))
                if j >= 2:
                    dve.wait_ge(max_step, count(b, 2 * (NJ - 1), half * (NJ - 1) + j - 1))
                before = scores[:, 0, :] if j == 1 else run_max[:]
                nc.vector.tensor_tensor(run_max[:], before, scores[:, j, :], ALU.max).then_inc(max_step, 1)

            def centre(b, half, j):
                dve.wait_ge(max_all, count(b, 2, half + 1))
                nc.vector.tensor_tensor(scores[:, j, :], scores[:, j, :], all_max[:], ALU.subtract).then_inc(centred, 1)

            def low_p(b, half, j):
                dve.wait_ge(p_high, count(b, 16, half * NJ + j + 1))
                nc.vector.tensor_tensor(p_lo[:, j, :], scores[:, j, :], p_hi[:, j, :].bitcast(F32),
                                        ALU.subtract).then_inc(p_split, 1)

            def add_up(b, half, j):
                if j >= 2:
                    dve.wait_ge(sum_step, count(b, 2 * (NJ - 1), half * (NJ - 1) + j - 1))
                before = scores[:, 0, :] if j == 1 else run_sum[:]
                nc.vector.tensor_tensor(run_sum[:], before, scores[:, j, :], ALU.add).then_inc(sum_step, 1)

            def inverse(b, half):
                dve.wait_ge(sum_all, count(b, 2, half + 1))
                nc.vector.reciprocal(inv_sum[:], inv_sum[:]).then_inc(inv_set, 1)

            def scale_out(b, n):
                half, c = divmod(n, KC)
                dve.wait_ge(o_summed, count(b, 8, n + 1))
                dve.wait_ge(out_stored[n % 2], count(b, 16 * KC, 16 * (n // 2 + 1)))
                dve.wait_ge(inv_set, count(b, 2, half + 1))
                nc.vector.tensor_tensor(stage[:, n % 2, :], o_bank(half, c)[:], inv_sum[:],
                                        ALU.mult).then_inc(o_scaled, 1)

            def add_residual(b, par, n):
                half, c = divmod(n, KC)
                dve.wait_ge(o_scaled, count(b, 8, 8 + n + 1))
                nc.vector.scalar_tensor_tensor(stage[:, n % 2, :], xt[:, par, c, half * HALF:(half + 1) * HALF],
                                               out_bias[:, c:c + 1], stage[:, n % 2, :], ALU.add,
                                               ALU.add).then_inc(o_done, 1)

            def next_h(b, par, n):
                dve.wait_ge(sum_step, count(b, 2 * (NJ - 1), NJ - 1 + max(n, 1)))
                low_h(b + 1, 1 - par, n, n)

            def outputs(b, par, half):
                for n in range(half * KC, (half + 1) * KC, 2):
                    scale_out(b, n)
                    scale_out(b, n + 1)
                    add_residual(b, par, n)
                    add_residual(b, par, n + 1)

            def batch(b, par, more):
                for c in range(KC):
                    low_t(b, 0, c)
                for j in range(NJ):
                    dve.wait_ge(v_high, count(b, 8, j + 1))
                    nc.vector.tensor_tensor(v_lo[:, j, :], v_bank(j)[:], v_hi[:, j, :].bitcast(F32),
                                            ALU.subtract).then_inc(v_split, 1)
                if more:
                    dve.wait_ge(x_in[1 - par], count(b, 8, 16 + 8 * par))
                for j in range(NJ):
                    if more:
                        bn_piece(b + 1, 1 - par, j)
                    if j >= 1:
                        if more and j == NJ - 1:
                            dve.wait_ge(bn_set, count(b, PIECES, 2 * PIECES))
                        maximum(b, 0, j)
                if more:
                    channel_stats(b + 1)
                centre(b, 0, 0)
                centre(b, 0, 1)
                for j in range(NJ):
                    if j in (1, 2, 4, 5):
                        low_t(b, 1, (1, 2, 4, 5).index(j))
                    if j == 2 and more:
                        group_spread(b + 1)
                    if j + 2 < NJ:
                        centre(b, 0, j + 2)
                    low_p(b, 0, j)
                    if j >= 1:
                        add_up(b, 0, j)
                inverse(b, 0)
                for j in range(1, NJ):
                    maximum(b, 1, j)
                if more:
                    group_variance(b + 1)
                centre(b, 1, 0)
                centre(b, 1, 1)
                if more:
                    affine(b + 1)
                for j in range(NJ):
                    if j + 2 < NJ:
                        centre(b, 1, j + 2)
                    low_p(b, 1, j)
                    if j >= 1:
                        add_up(b, 1, j)
                    if more and j >= 2:
                        next_h(b, par, j - 2)
                if more:
                    next_h(b, par, NJ - 2)
                    next_h(b, par, NJ - 1)
                outputs(b, par, 0)
                inverse(b, 1)
                outputs(b, par, 1)

            images(dve, batch)


_TAKEN = {"x": "x", "L0_conv_norm_gamma": "gamma", "L0_conv_norm_beta": "beta", "L0_conv_wq": "wq",
          "L0_conv_bq": "bq", "L0_conv_wk": "wk", "L0_conv_wv": "wv", "L0_conv_bv": "bv",
          "L0_conv_wo": "wo", "L0_conv_bo": "bo"}


def kernel(**inputs):
    import numpy as np
    import concourse.bacc as bacc
    from concourse.bass_utils import run_bass_kernel_spmd

    nc = bacc.Bacc("TRN2", target_bir_lowering=False, num_devices=1)
    arrays, args = {}, {}
    for name, short in _TAKEN.items():
        a = np.ascontiguousarray(inputs[name])
        arrays[f"in_{short}"] = a
        args[short] = nc.dram_tensor(f"in_{short}", a.shape, mybir.dt.from_np(a.dtype), kind="ExternalInput").ap()
    shape = arrays["in_x"].shape
    args["out"] = nc.dram_tensor("out", shape, F32, kind="ExternalOutput").ap()
    attention_program(nc, **args)
    r = run_bass_kernel_spmd(nc, [arrays], core_ids=[0])
    return r.results[0]["out"]
```

```python
from contextlib import ExitStack

import concourse.bass as bass
from concourse import mybir

F32 = mybir.dt.float32
F32R = mybir.dt.float32r
ALU = mybir.AluOpType
ACT = mybir.ActivationFunctionType
MAX_ALL = bass.bass_isa.ReduceOp.max
ADD_ALL = bass.bass_isa.ReduceOp.add

P = 128
GROUPS = 32
EPS = 1e-6


def attention_program(nc, x, gamma, beta, wq, bq, wk, wv, bv, wo, bo, out):
    B, C, H, W = x.shape
    N = H * W
    KC = C // P
    NJ = N // P
    HALF = N // 2
    CG = C // GROUPS
    SCALE = float(C) ** -0.5
    PIECES = N * KC // HALF
    assert HALF == 512 and C == 512 and NJ == 2 * KC and P % CG == 0 and B % 2 == 0 and B >= 4

    x_d = x.rearrange("b (k p) h w -> b p k (h w)", p=P)
    out_d = out.rearrange("b (k p) h w -> b k p (h w)", p=P)
    w_d = {n: a.rearrange("(k p) n -> p k n", p=P) for n, a in (("q", wq), ("k", wk), ("v", wv), ("o", wo))}
    bq_d, *vec_d = [a.rearrange("(k p) -> p k", p=P) for a in (bq, gamma, beta, bo)]

    with ExitStack() as ctx:
        def sb(name, shape, dt=F32):
            return ctx.enter_context(nc.sbuf_tensor(name, [P, *shape], dt))

        def sem(name):
            return ctx.enter_context(nc.semaphore(name))

        wkq_hi, wkq_lo = sb("wkq_hi", [KC, C], F32R), sb("wkq_lo", [KC, C], F32R)
        wov_hi, wov_lo = sb("wov_hi", [KC, C], F32R), sb("wov_lo", [KC, C], F32R)
        h_hi, h_lo = sb("h_hi", [KC, N], F32R), sb("h_lo", [KC, N], F32R)
        t_hi, t_lo = sb("t_hi", [KC, HALF], F32R), sb("t_lo", [KC, HALF], F32R)
        v_hi, v_lo = sb("v_hi", [NJ, C], F32R), sb("v_lo", [NJ, C], F32R)
        p_hi, p_lo = sb("p_hi", [NJ, HALF], F32R), sb("p_lo", [NJ, HALF], F32R)
        xt = sb("xt", [2, KC, N])
        scores = sb("scores", [NJ, HALF])
        stage = sb("stage", [2, HALF])
        run_max, all_max = sb("run_max", [HALF]), sb("all_max", [HALF])
        run_sum, inv_sum = sb("run_sum", [HALF]), sb("inv_sum", [HALF])
        ident, group_mean = sb("ident", [P]), sb("group_mean", [P])
        bq_s, vecs = sb("bq_s", [KC]), sb("vecs", [3, KC])
        gamma_s, beta_s, bo_s = (vecs[:, n, :] for n in range(3))
        t_bias, out_bias, wo_bv = sb("t_bias", [KC]), sb("out_bias", [KC]), sb("wo_bv", [KC])
        bn = sb("bn", [PIECES, 6])
        chan = sb("chan", [KC, 2])
        mean_g, diff, spread = sb("mean_g", [KC]), sb("diff", [KC]), sb("spread", [KC])
        var_g, rstd, minus_half = sb("var_g", [KC]), sb("rstd", [KC]), sb("minus_half", [KC])
        h_scale, h_shift, shift0 = sb("h_scale", [KC]), sb("h_shift", [KC]), sb("shift0", [KC])

        wq_raw, wk_raw = scores[:, 0:KC, :], scores[:, KC:2 * KC, :]
        raw = xt[:, 1, :, :].rearrange("p k n -> p (k n)")
        wv_raw = raw[:, 0:KC * C].rearrange("p (k n) -> p k n", k=KC)
        wo_raw = raw[:, KC * C:2 * KC * C].rearrange("p (k n) -> p k n", k=KC)
        wq_hi, wq_lo, wk_hi, wk_lo = v_hi[:, 0:KC, :], v_lo[:, 0:KC, :], v_hi[:, KC:NJ, :], v_lo[:, KC:NJ, :]
        wv_hi, wv_lo, wot_hi, wot_lo = p_hi[:, 0:KC, :], p_lo[:, 0:KC, :], p_hi[:, KC:NJ, :], p_lo[:, KC:NJ, :]
        bv_rows, wo_bv_terms = stage[:, 0, :], stage[:, 1, :]
        wk_bq_terms, t_bias_rows = run_max[:], all_max[:]

        bank = [ctx.enter_context(nc.psum_tensor(f"bank{n}", [P, 512], F32)) for n in range(8)]

        def t_bank(half, c):
            return bank[4 * half + c]

        def v_bank(j):
            return bank[(4 + j) % 8]

        def s_bank(half, j):
            return bank[j if half else (4 + j) % 8]

        def o_bank(half, c):
            return bank[4 * half + c]

        MEAN_BANK, VAR_BANK = bank[3], bank[4]

        wv_in, wo_in, bq_in, vec_in, bv_in = (sem(n) for n in ("wv_in", "wo_in", "bq_in", "vec_in", "bv_in"))
        wk_in = [sem(f"wk_in{o}") for o in range(KC)]
        wq_in = [sem(f"wq_in{o}") for o in range(KC)]
        x0_in = [sem(f"x0_in{k}") for k in range(KC)]
        x_in = [sem("x_in0"), sem("x_in1")]
        out_stored = [sem("out_stored0"), sem("out_stored1")]
        consts_set, max_all, sum_all, rstd_set = (sem(n) for n in ("consts_set", "max_all", "sum_all", "rstd_set"))
        reduce_begun = sem("reduce_begun")
        wkq_summed, wov_summed, wo_turned = (sem(n) for n in ("wkq_summed", "wov_summed", "wo_turned"))
        t_summed, v_summed, s_summed, o_summed = (sem(n) for n in ("t_summed", "v_summed", "s_summed", "o_summed"))
        mean_summed, var_summed, p_used = (sem(n) for n in ("mean_summed", "var_summed", "p_used"))
        wk_high, wq_high, wv_high, wot_high, wkq_high, wov_high = (
            sem(n) for n in ("wk_high", "wq_high", "wv_high", "wot_high", "wkq_high", "wov_high"))
        t_high, v_high, h_high, p_high, s_copied, exp_set = (
            sem(n) for n in ("t_high", "v_high", "h_high", "p_high", "s_copied", "exp_set"))
        wk_split, wq_split, wv_split, wot_split, wkq_split, wov_split = (
            sem(n) for n in ("wk_split", "wq_split", "wv_split", "wot_split", "wkq_split", "wov_split"))
        bq_step, bq_summed, bv_used, diagonals_set, biases_set, t_split, v_split, h_split, p_split = (
            sem(n) for n in ("bq_step", "bq_summed", "bv_used", "diagonals_set", "biases_set", "t_split", "v_split", "h_split", "p_split"))
        max_step, centred, sum_step, inv_set = (sem(n) for n in ("max_step", "centred", "sum_step", "inv_set"))
        bn_set, chan_set, mean_step, spread_set, var_set, scale_step, h_full = (
            sem(n) for n in ("bn_set", "chan_set", "mean_step", "spread_set", "var_set", "scale_step", "h_full"))
        o_scaled, o_done = sem("o_scaled"), sem("o_done")

        block = ctx.enter_context(nc.Block())

        def images(engine, batch):
            with engine.Fori(0, B - 2, 2) as b:
                batch(b, 0, True)
                batch(b + 1, 1, True)
            batch(B - 2, 0, True)
            batch(B - 1, 1, False)

        def count(b, per_image, step):
            return b * per_image + step

        @block.sync
        def _(sp):
            for o in range(KC):
                sp.dma_start(wk_raw[:, o, :], w_d["k"][:, o, :]).then_inc(wk_in[o], 16)
                sp.dma_start(wq_raw[:, o, :], w_d["q"][:, o, :]).then_inc(wq_in[o], 16)
            sp.dma_start(wo_raw, w_d["o"]).then_inc(wo_in, 16)
            sp.dma_start(wv_raw, w_d["v"]).then_inc(wv_in, 16)
            for k in range(KC):
                sp.dma_start(xt[:, 0, k, :], x_d[0][:, k, :]).then_inc(x0_in[k], 16)
            for s in range(2):
                sp.sem_inc(out_stored[s], 16)

            def batch(b, par, more):
                if more:
                    sp.wait_ge(o_done, count(b, 8, 8))
                    sp.dma_start(xt[:, 1 - par, :, :], x_d[b + 1]).then_inc(x_in[1 - par], 16)
                for n in range(2 * KC):
                    half, c = divmod(n, KC)
                    sp.wait_ge(o_done, count(b, 8, 8 + n + 1))
                    sp.dma_start(out_d[b, c, :, half * HALF:(half + 1) * HALF],
                                 stage[:, n % 2, :]).then_inc(out_stored[n % 2], 16)

            images(sp, batch)
            for s in range(2):
                sp.wait_ge(out_stored[s], 16 * (1 + B * KC))

        @block.gpsimd
        def _(pool):
            nc.gpsimd.memset(ident[:], 0.0).then_inc(consts_set, 1)
            nc.gpsimd.memset(group_mean[:], 1.0 / CG).then_inc(consts_set, 1)
            nc.gpsimd.memset(minus_half[:], -0.5).then_inc(consts_set, 1)
            pool.wait_ge(consts_set, 3)
            nc.gpsimd.affine_select(out=ident[:], in_=ident[:], compare_op=ALU.not_equal, fill=1.0, base=0,
                                    pattern=[[-1, P]], channel_multiplier=1).then_inc(consts_set, 1)
            blocks = group_mean[:].rearrange("p (g d) -> p g d", d=CG)
            nc.gpsimd.affine_select(out=blocks, in_=blocks, compare_op=ALU.is_ge, fill=0.0, base=0,
                                    pattern=[[-CG, P // CG], [0, CG]], channel_multiplier=1).then_inc(consts_set, 1)
            pool.wait_ge(consts_set, 5)
            nc.gpsimd.affine_select(out=blocks, in_=blocks, compare_op=ALU.is_ge, fill=0.0, base=CG - 1,
                                    pattern=[[CG, P // CG], [0, CG]], channel_multiplier=-1).then_inc(consts_set, 1)

            for o in range(KC):
                pool.wait_ge(wv_high, o + 1)
                nc.gpsimd.tensor_tensor(wv_lo[:, o, :], wv_raw[:, o, :], wv_hi[:, o, :].bitcast(F32),
                                        ALU.subtract).then_inc(wv_split, 1)

            pool.wait_ge(bq_step, KC)
            nc.gpsimd.partition_all_reduce(t_bias_rows, wk_bq_terms, P, ADD_ALL).then_inc(bq_summed, 1)

            def deviation(b):
                pool.wait_ge(var_set, count(b, 1, 1))
                nc.gpsimd.tensor_tensor(rstd[:], var_g[:], minus_half[:], ALU.pow).then_inc(rstd_set, 1)

            deviation(0)
            def batch(b, par, more):
                for half in range(2):
                    pool.wait_ge(max_step, count(b, 2 * (NJ - 1), (half + 1) * (NJ - 1)))
                    pool.sem_inc(reduce_begun, 1)
                    nc.gpsimd.partition_all_reduce(all_max[:], run_max[:], P, MAX_ALL).then_inc(max_all, 1)
                    if half and more:
                        deviation(b + 1)
                    pool.wait_ge(sum_step, count(b, 2 * (NJ - 1), (half + 1) * (NJ - 1)))
                    pool.wait_ge(o_scaled, count(b, 8, 8 + half * KC))
                    pool.sem_inc(reduce_begun, 1)
                    nc.gpsimd.partition_all_reduce(inv_sum[:], run_sum[:], P, ADD_ALL).then_inc(sum_all, 1)

            images(pool, batch)

        @block.tensor
        def _(pe):
            def product(o, a_hi, a_lo, b_hi, b_lo, start, stop):
                nc.tensor.matmul(o, a_hi, b_hi, start=start, stop=False)
                nc.tensor.matmul(o, a_hi, b_lo, start=False, stop=False)
                return nc.tensor.matmul(o, a_lo, b_hi, start=False, stop=stop)

            def cols(n):
                return slice(n * P, (n + 1) * P)

            def group_means(bk, values):
                return nc.tensor.matmul(bk[:, 0:KC], group_mean[:], values, start=True, stop=True)

            for o in range(KC):
                pe.wait_ge(wk_split, o + 1)
                pe.wait_ge(wq_split, o + 1)
                for c in range(KC):
                    mm = product(bank[c][:], wq_hi[:, o, cols(c)], wq_lo[:, o, cols(c)],
                                 wk_hi[:, o, :], wk_lo[:, o, :], o == 0, o == KC - 1)
                    if o == KC - 1:
                        mm.then_inc(wkq_summed, 1)
                if o == KC - 2:
                    pe.wait_ge(wo_in, 16)
                    pe.wait_ge(consts_set, 6)
                    for n in range(KC):
                        for c in range(KC):
                            mm = nc.tensor.transpose(bank[4 + n][:, cols(c)], wo_raw[:, c, cols(n)], ident[:])
                        mm.then_inc(wo_turned, 1)
            for c in range(KC):
                pe.wait_ge(wot_split, KC)
                for o in range(KC):
                    pe.wait_ge(wv_split, o + 1)
                    mm = product(bank[4 + c][:], wv_hi[:, o, cols(c)], wv_lo[:, o, cols(c)],
                                 wot_hi[:, o, :], wot_lo[:, o, :], o == 0, o == KC - 1)
                    if (c, o) == (1, 1):
                        pe.wait_ge(chan_set, KC)
                        group_means(bank[7], chan[:, :, 0]).then_inc(mean_summed, 1)
                    if (c, o) == (1, 3):
                        pe.wait_ge(spread_set, 1)
                        group_means(bank[6], spread[:]).then_inc(var_summed, 1)
                        pe.wait_ge(var_set, 1)
                mm.then_inc(wov_summed, 1)

            def t_part(half, c, k):
                q = slice(half * HALF, (half + 1) * HALF)
                return product(t_bank(half, c)[:], wkq_hi[:, k, cols(c)], wkq_lo[:, k, cols(c)],
                               h_hi[:, k, q], h_lo[:, k, q], k == 0, k == KC - 1)

            def make_t_0(b):
                for k in range(KC):
                    pe.wait_ge(h_split, count(b, PIECES, 2 * (k + 1)))
                    for c in range(KC):
                        if k == 0:
                            pe.wait_ge(o_scaled, count(b, 8, c + 1))
                        mm = t_part(0, c, k)
                        if k == KC - 1:
                            mm.then_inc(t_summed, 1)

            def make_t_1(b, more):
                for c in range(KC):
                    pe.wait_ge(s_copied, count(b, 16, c + 1))
                    for k in range(KC):
                        mm = t_part(1, c, k)
                    mm.then_inc(t_summed, 1)
                    if more and c == 1:
                        pe.wait_ge(chan_set, count(b, KC, 2 * KC))
                        pe.wait_ge(s_copied, count(b, 16, NJ))
                        group_means(MEAN_BANK, chan[:, :, 0]).then_inc(mean_summed, 1)

            def make_v(b):
                for j in range(NJ):
                    if j < 4:
                        pe.wait_ge(o_scaled, count(b, 8, 4 + j + 1))
                    else:
                        pe.wait_ge(t_split, count(b, 8, j - 4 + 1))
                    for k in range(KC):
                        if j == 0:
                            pe.wait_ge(wov_split, k + 1)
                        mm = product(v_bank(j)[:], h_hi[:, k, cols(j)], h_lo[:, k, cols(j)],
                                     wov_hi[:, k, :], wov_lo[:, k, :], k == 0, k == KC - 1)
                    mm.then_inc(v_summed, 1)

            def score(half, j, k):
                return product(s_bank(half, j)[:], h_hi[:, k, cols(j)], h_lo[:, k, cols(j)],
                               t_hi[:, k, :], t_lo[:, k, :], k == 0, k == KC - 1)

            def scores_0(b):
                pe.wait_ge(t_split, count(b, 8, KC))
                for j in range(NJ):
                    pe.wait_ge(v_split, count(b, 8, j + 1))
                    for k in range(KC):
                        mm = score(0, j, k)
                    mm.then_inc(s_summed, 1)

            def scores_1(b, more):
                for k in range(KC):
                    pe.wait_ge(t_split, count(b, 8, KC + k + 1))
                    for j in range(4):
                        if k == 0:
                            pe.wait_ge(s_copied, count(b, 16, j + 4 + 1))
                            if more and s_bank(1, j) is MEAN_BANK:
                                pe.wait_ge(mean_step, count(b, 3, 3 + 1))
                        mm = score(1, j, k)
                        if k == KC - 1:
                            mm.then_inc(s_summed, 1)
                for j in range(4, NJ):
                    for k in range(KC):
                        mm = score(1, j, k)
                    mm.then_inc(s_summed, 1)

            def last_outputs(b):
                for c in range(KC):
                    pe.wait_ge(s_copied, count(b, 16, NJ + 4 + c + 1))
                    for j in range(NJ):
                        if c == 0:
                            pe.wait_ge(p_split, count(b, 16, NJ + j + 1))
                        mm = product(o_bank(1, c)[:], v_hi[:, j, cols(c)], v_lo[:, j, cols(c)],
                                     p_hi[:, j, :], p_lo[:, j, :], j == 0, j == NJ - 1)
                    mm.then_inc(o_summed, 1)

            def outputs(b, half, more):
                for j in range(NJ):
                    pe.wait_ge(p_split, count(b, 16, half * NJ + j + 1))
                    for c in range(KC):
                        if j == 0:
                            pe.wait_ge(s_copied, count(b, 16, NJ + 4 * half + c + 1))
                            if more and o_bank(half, c) is VAR_BANK:
                                pe.wait_ge(var_set, count(b, 1, 2))
                        mm = product(o_bank(half, c)[:], v_hi[:, j, cols(c)], v_lo[:, j, cols(c)],
                                     p_hi[:, j, :], p_lo[:, j, :], j == 0, j == NJ - 1)
                        if j == NJ - 1:
                            mm.then_inc(o_summed, 1)
                    if half == 0 and j < NJ - 1:
                        mm.then_inc(p_used, 1)

            def batch(b, par, more):
                make_t_0(b)
                make_v(b)
                scores_0(b)
                make_t_1(b, more)
                scores_1(b, more)
                if more:
                    pe.wait_ge(spread_set, count(b, 1, 2))
                    pe.wait_ge(s_copied, count(b, 16, NJ + 4 + 1))
                    group_means(VAR_BANK, spread[:]).then_inc(var_summed, 1)
                pe.wait_ge(v_split, count(b, 8, NJ))
                outputs(b, 0, more)
                if more:
                    outputs(b, 1, more)
                else:
                    last_outputs(b)

            images(pe, batch)

        @block.scalar
        def _(act):
            act.dma_start(bq_s[:], bq_d, allow_slow_non_contiguous=True).then_inc(bq_in, 16)
            nc.scalar.preload_act_table(ACT.Exp)
            for o in range(KC):
                act.wait_ge(wk_in[o], 16)
                nc.scalar.copy(wk_hi[:, o, :], wk_raw[:, o, :]).then_inc(wk_high, 1)
                act.wait_ge(wq_in[o], 16)
                nc.scalar.copy(wq_hi[:, o, :], wq_raw[:, o, :]).then_inc(wq_high, 1)
                if o == 1:
                    for n, a in enumerate(vec_d):
                        act.dma_start(vecs[:, n, :], a, allow_slow_non_contiguous=True).then_inc(vec_in, 16)
                    act.dma_start(bv_rows, bv.partition_broadcast(P)).then_inc(bv_in, 16)
            act.wait_ge(wv_in, 16)
            for o in range(KC):
                nc.scalar.copy(wv_hi[:, o, :], wv_raw[:, o, :]).then_inc(wv_high, 1)
            for o in range(KC):
                act.wait_ge(wo_turned, o + 1)
                nc.scalar.copy(wot_hi[:, o, :], bank[4 + o][:]).then_inc(wot_high, 1)
            for c in range(KC):
                act.wait_ge(wkq_summed, c + 1)
                nc.scalar.copy(wkq_hi[:, c, :], bank[c][:]).then_inc(wkq_high, 1)

            def high_h(b, par, k):
                act.wait_ge(scale_step, count(b, 3, 3))
                nc.scalar.activation(h_hi[:, k, :], xt[:, par, k, :], ACT.Identity, bias=h_shift[:, k:k + 1],
                                     scale=h_scale[:, k:k + 1]).then_inc(h_high, 1)

            for k in range(KC):
                high_h(0, 0, k)
            for c in range(KC):
                act.wait_ge(wov_summed, c + 1)
                nc.scalar.copy(wov_hi[:, c, :], bank[4 + c][:]).then_inc(wov_high, 1)

            act.wait_ge(diagonals_set, KC)

            def high_t(b, half, c):
                act.wait_ge(t_summed, count(b, 8, half * KC + c + 1))
                nc.scalar.activation(t_hi[:, c, :], t_bank(half, c)[:], ACT.Identity,
                                     bias=t_bias[:, c:c + 1]).then_inc(t_high, 1)

            def copy_scores(b, half, j):
                act.wait_ge(s_summed, count(b, 16, half * NJ + j + 1))
                if half == 0:
                    act.wait_ge(h_split, count(b, PIECES, j + 1))
                else:
                    act.wait_ge(sum_step, count(b, 2 * (NJ - 1), max(j, 1)))
                nc.scalar.copy(scores[:, j, :], s_bank(half, j)[:]).then_inc(s_copied, 1)

            def exponentials(b, half, j):
                act.wait_ge(centred, count(b, 16, half * NJ + j + 1))
                nc.scalar.activation(scores[:, j, :], scores[:, j, :], ACT.Exp, scale=SCALE).then_inc(exp_set, 1)

            def high_p(b, half, j):
                act.wait_ge(exp_set, count(b, 16, half * NJ + j + 1))
                if half == 1 and j < NJ - 1:
                    act.wait_ge(p_used, count(b, NJ - 1, j + 1))
                elif half == 1:
                    act.wait_ge(o_summed, count(b, 8, KC))
                nc.scalar.copy(p_hi[:, j, :], scores[:, j, :]).then_inc(p_high, 1)

            def batch(b, par, more):
                for c in range(KC):
                    high_t(b, 0, c)
                for j in range(NJ):
                    act.wait_ge(v_summed, count(b, 8, j + 1))
                    nc.scalar.copy(v_hi[:, j, :], v_bank(j)[:]).then_inc(v_high, 1)
                for j in range(NJ):
                    copy_scores(b, 0, j)
                high_t(b, 1, 0)
                exponentials(b, 0, 0)
                for j in range(NJ):
                    if 1 <= j < KC:
                        high_t(b, 1, j)
                    if j + 1 < NJ:
                        exponentials(b, 0, j + 1)
                    high_p(b, 0, j)
                for j in range(NJ):
                    copy_scores(b, 1, j)
                exponentials(b, 1, 0)
                for j in range(NJ):
                    if j + 1 < NJ:
                        exponentials(b, 1, j + 1)
                    high_p(b, 1, j)
                    if more and j < KC:
                        high_h(b + 1, 1 - par, j)

            images(act, batch)

        @block.vector
        def _(dve):
            def piece_of(par, n):
                k, half = divmod(n, 2)
                return k, xt[:, par, k, half * HALF:(half + 1) * HALF]

            def bn_piece(b, par, n):
                k, piece = piece_of(par, n)
                nc.vector.bn_stats(bn[:, n, :], piece).then_inc(bn_set, 1)

            def channel_stats(b):
                for k in range(KC):
                    nc.vector.bn_aggr(chan[:, k, :],
                                       bn[:, 2 * k:2 * k + 2, :].rearrange("p a s -> p (a s)")).then_inc(chan_set, 1)

            def group_spread(b, means=MEAN_BANK):
                dve.wait_ge(mean_summed, count(b, 1, 1))
                nc.vector.tensor_copy(mean_g[:], means[:, 0:KC]).then_inc(mean_step, 1)
                dve.wait_ge(mean_step, count(b, 3, 1))
                dve.wait_ge(chan_set, count(b, KC, KC))
                nc.vector.tensor_tensor(diff[:], chan[:, :, 0], mean_g[:], ALU.subtract).then_inc(mean_step, 1)
                dve.wait_ge(mean_step, count(b, 3, 2))
                nc.vector.tensor_tensor(diff[:], diff[:], diff[:], ALU.mult).then_inc(mean_step, 1)
                dve.wait_ge(mean_step, count(b, 3, 3))
                nc.vector.tensor_tensor(spread[:], diff[:], chan[:, :, 1], ALU.add).then_inc(spread_set, 1)

            def group_variance(b, variances=VAR_BANK):
                dve.wait_ge(var_summed, count(b, 1, 1))
                nc.vector.tensor_scalar(var_g[:], variances[:, 0:KC], EPS, None, ALU.add).then_inc(var_set, 1)

            def affine(b):
                dve.wait_ge(rstd_set, count(b, 1, 1))
                nc.vector.tensor_tensor(h_scale[:], gamma_s, rstd[:], ALU.mult).then_inc(scale_step, 1)
                dve.wait_ge(scale_step, count(b, 3, 1))
                nc.vector.tensor_tensor(shift0[:], mean_g[:], h_scale[:], ALU.mult).then_inc(scale_step, 1)
                dve.wait_ge(scale_step, count(b, 3, 2))
                nc.vector.tensor_tensor(h_shift[:], beta_s, shift0[:], ALU.subtract).then_inc(scale_step, 1)

            def low_h(b, par, n, slot):
                k, piece = piece_of(par, n)
                dve.wait_ge(scale_step, count(b, 3, 3))
                nc.vector.tensor_scalar(scores[:, slot, :], piece, h_scale[:, k:k + 1], h_shift[:, k:k + 1],
                                        ALU.mult, ALU.add).then_inc(h_full, 1)
                q = slice((n % 2) * HALF, (n % 2 + 1) * HALF)
                dve.wait_ge(h_full, count(b, PIECES, n + 1))
                dve.wait_ge(h_high, count(b, KC, k + 1))
                nc.vector.tensor_tensor(h_lo[:, k, q], scores[:, slot, :], h_hi[:, k, q].bitcast(F32),
                                        ALU.subtract).then_inc(h_split, 1)

            for o in range(KC):
                dve.wait_ge(wk_high, o + 1)
                nc.vector.tensor_tensor(wk_lo[:, o, :], wk_raw[:, o, :], wk_hi[:, o, :].bitcast(F32),
                                        ALU.subtract).then_inc(wk_split, 1)
                dve.wait_ge(wq_high, o + 1)
                nc.vector.tensor_tensor(wq_lo[:, o, :], wq_raw[:, o, :], wq_hi[:, o, :].bitcast(F32),
                                        ALU.subtract).then_inc(wq_split, 1)
            dve.wait_ge(bq_in, 16)
            nc.vector.tensor_scalar(wk_bq_terms, wk_raw[:, 0, :], bq_s[:, 0:1], None, ALU.mult).then_inc(bq_step, 1)
            for o in range(1, KC):
                dve.wait_ge(bq_step, o)
                nc.vector.scalar_tensor_tensor(wk_bq_terms, wk_raw[:, o, :], bq_s[:, o:o + 1], wk_bq_terms,
                                               ALU.mult, ALU.add).then_inc(bq_step, 1)
            for n in range(PIECES):
                dve.wait_ge(x0_in[n // 2], 16)
                bn_piece(0, 0, n)
                if n == 1:
                    for o in range(KC):
                        dve.wait_ge(wot_high, o + 1)
                        nc.vector.tensor_tensor(wot_lo[:, o, :], bank[4 + o][:], wot_hi[:, o, :].bitcast(F32),
                                                ALU.subtract).then_inc(wot_split, 1)
            dve.wait_ge(bn_set, PIECES)
            channel_stats(0)
            dve.wait_ge(wkq_high, 1)
            nc.vector.tensor_tensor(wkq_lo[:, 0, :], bank[0][:], wkq_hi[:, 0, :].bitcast(F32),
                                    ALU.subtract).then_inc(wkq_split, 1)
            group_spread(0, bank[7])
            group_variance(0, bank[6])
            for c in range(1, KC):
                dve.wait_ge(wkq_high, c + 1)
                nc.vector.tensor_tensor(wkq_lo[:, c, :], bank[c][:], wkq_hi[:, c, :].bitcast(F32),
                                        ALU.subtract).then_inc(wkq_split, 1)
            dve.wait_ge(vec_in, 16 * len(vec_d))
            affine(0)
            dve.wait_ge(wkq_split, KC)
            dve.sem_inc(o_scaled, 4)
            for n in range(PIECES):
                low_h(0, 0, n, n)
            dve.wait_ge(bq_summed, 1)
            dve.wait_ge(consts_set, 6)
            for c in range(KC):
                if c:
                    dve.wait_ge(diagonals_set, c)
                nc.vector.tensor_tensor_reduce(out=wk_bq_terms[:, 0:P], in0=t_bias_rows[:, c * P:(c + 1) * P],
                                               in1=ident[:], scale=1.0, scalar=0.0, op0=ALU.mult, op1=ALU.add,
                                               accum_out=t_bias[:, c:c + 1]).then_inc(diagonals_set, 1)
            for c in range(KC):
                dve.wait_ge(wov_high, c + 1)
                nc.vector.tensor_tensor(wov_lo[:, c, :], bank[4 + c][:], wov_hi[:, c, :].bitcast(F32),
                                        ALU.subtract).then_inc(wov_split, 1)
            dve.wait_ge(diagonals_set, KC)
            dve.wait_ge(wov_split, KC)
            dve.sem_inc(o_scaled, 4)
            dve.wait_ge(bv_in, 16)
            for c in range(KC):
                if c:
                    dve.wait_ge(bv_used, c)
                nc.vector.tensor_tensor_reduce(out=wo_bv_terms, in0=wo_raw[:, c, :], in1=bv_rows, scale=1.0,
                                               scalar=0.0, op0=ALU.mult, op1=ALU.add,
                                               accum_out=wo_bv[:, c:c + 1]).then_inc(bv_used, 1)
            dve.wait_ge(bv_used, KC)
            nc.vector.tensor_tensor(out_bias[:], wo_bv[:], bo_s, ALU.add).then_inc(biases_set, 1)
            dve.wait_ge(biases_set, 1)
            dve.sem_inc(o_done, 8)

            def low_t(b, half, c):
                dve.wait_ge(t_high, count(b, 8, half * KC + c + 1))
                nc.vector.scalar_tensor_tensor(t_lo[:, c, :], t_bank(half, c)[:], t_bias[:, c:c + 1],
                                               t_hi[:, c, :].bitcast(F32), ALU.add, ALU.subtract).then_inc(t_split, 1)

            def maximum(b, half, j):
                dve.wait_ge(s_copied, count(b, 16, half * NJ + j + 1))
                if j >= 2:
                    dve.wait_ge(max_step, count(b, 2 * (NJ - 1), half * (NJ - 1) + j - 1))
                before = scores[:, 0, :] if j == 1 else run_max[:]
                nc.vector.tensor_tensor(run_max[:], before, scores[:, j, :], ALU.max).then_inc(max_step, 1)

            def centre(b, half, j):
                dve.wait_ge(max_all, count(b, 2, half + 1))
                nc.vector.tensor_tensor(scores[:, j, :], scores[:, j, :], all_max[:], ALU.subtract).then_inc(centred, 1)

            def low_p(b, half, j):
                dve.wait_ge(p_high, count(b, 16, half * NJ + j + 1))
                nc.vector.tensor_tensor(p_lo[:, j, :], scores[:, j, :], p_hi[:, j, :].bitcast(F32),
                                        ALU.subtract).then_inc(p_split, 1)

            def add_up(b, half, j):
                if j >= 2:
                    dve.wait_ge(sum_step, count(b, 2 * (NJ - 1), half * (NJ - 1) + j - 1))
                before = scores[:, 0, :] if j == 1 else run_sum[:]
                nc.vector.tensor_tensor(run_sum[:], before, scores[:, j, :], ALU.add).then_inc(sum_step, 1)

            def inverse(b, half):
                dve.wait_ge(sum_all, count(b, 2, half + 1))
                nc.vector.reciprocal(inv_sum[:], inv_sum[:]).then_inc(inv_set, 1)

            def scale_out(b, n):
                half, c = divmod(n, KC)
                dve.wait_ge(o_summed, count(b, 8, n + 1))
                dve.wait_ge(out_stored[n % 2], count(b, 16 * KC, 16 * (n // 2 + 1)))
                dve.wait_ge(inv_set, count(b, 2, half + 1))
                nc.vector.tensor_tensor(stage[:, n % 2, :], o_bank(half, c)[:], inv_sum[:],
                                        ALU.mult).then_inc(o_scaled, 1)

            def add_residual(b, par, n):
                half, c = divmod(n, KC)
                dve.wait_ge(o_scaled, count(b, 8, 8 + n + 1))
                nc.vector.scalar_tensor_tensor(stage[:, n % 2, :], xt[:, par, c, half * HALF:(half + 1) * HALF],
                                               out_bias[:, c:c + 1], stage[:, n % 2, :], ALU.add,
                                               ALU.add).then_inc(o_done, 1)

            def next_h(b, par, n):
                dve.wait_ge(sum_step, count(b, 2 * (NJ - 1), NJ - 1 + max(n, 1)))
                low_h(b + 1, 1 - par, n, n)

            def outputs(b, par, half):
                for n in range(half * KC, (half + 1) * KC, 2):
                    scale_out(b, n)
                    scale_out(b, n + 1)
                    add_residual(b, par, n)
                    add_residual(b, par, n + 1)

            def batch(b, par, more):
                for c in range(KC):
                    low_t(b, 0, c)
                for j in range(NJ):
                    dve.wait_ge(v_high, count(b, 8, j + 1))
                    nc.vector.tensor_tensor(v_lo[:, j, :], v_bank(j)[:], v_hi[:, j, :].bitcast(F32),
                                            ALU.subtract).then_inc(v_split, 1)
                if more:
                    dve.wait_ge(x_in[1 - par], count(b, 8, 16 - 8 * par))
                for j in range(NJ):
                    if more:
                        bn_piece(b + 1, 1 - par, j)
                    if j >= 1:
                        if more and j == NJ - 1:
                            dve.wait_ge(bn_set, count(b, PIECES, 2 * PIECES))
                        maximum(b, 0, j)
                if more:
                    channel_stats(b + 1)
                centre(b, 0, 0)
                centre(b, 0, 1)
                for j in range(NJ):
                    if 1 <= j <= KC:
                        low_t(b, 1, j - 1)
                    if j == 2 and more:
                        group_spread(b + 1)
                    if j + 2 < NJ:
                        centre(b, 0, j + 2)
                    low_p(b, 0, j)
                    if j >= 1:
                        add_up(b, 0, j)
                inverse(b, 0)
                for j in range(1, NJ):
                    maximum(b, 1, j)
                if more:
                    group_variance(b + 1)
                centre(b, 1, 0)
                centre(b, 1, 1)
                if more:
                    affine(b + 1)
                for j in range(NJ):
                    if j + 2 < NJ:
                        centre(b, 1, j + 2)
                    low_p(b, 1, j)
                    if j >= 1:
                        add_up(b, 1, j)
                    if more and j >= 2:
                        next_h(b, par, j - 2)
                if more:
                    next_h(b, par, NJ - 2)
                    next_h(b, par, NJ - 1)
                outputs(b, par, 0)
                inverse(b, 1)
                if more:
                    outputs(b, par, 1)
                else:
                    for n in range(KC, 2 * KC):
                        scale_out(b, n)
                        add_residual(b, par, n)

            images(dve, batch)


_TAKEN = {"x": "x", "L0_conv_norm_gamma": "gamma", "L0_conv_norm_beta": "beta", "L0_conv_wq": "wq",
          "L0_conv_bq": "bq", "L0_conv_wk": "wk", "L0_conv_wv": "wv", "L0_conv_bv": "bv",
          "L0_conv_wo": "wo", "L0_conv_bo": "bo"}


def kernel(**inputs):
    import numpy as np
    import concourse.bacc as bacc
    from concourse.bass_utils import run_bass_kernel_spmd

    nc = bacc.Bacc("TRN2", target_bir_lowering=False, num_devices=1)
    arrays, args = {}, {}
    for name, short in _TAKEN.items():
        a = np.ascontiguousarray(inputs[name])
        arrays[f"in_{short}"] = a
        args[short] = nc.dram_tensor(f"in_{short}", a.shape, mybir.dt.from_np(a.dtype), kind="ExternalInput").ap()
    shape = arrays["in_x"].shape
    args["out"] = nc.dram_tensor("out", shape, F32, kind="ExternalOutput").ap()
    attention_program(nc, **args)
    r = run_bass_kernel_spmd(nc, [arrays], core_ids=[0])
    return r.results[0]["out"]
```

```python
from contextlib import ExitStack

import concourse.bass as bass
from concourse import mybir

F32 = mybir.dt.float32
F32R = mybir.dt.float32r
ALU = mybir.AluOpType
ACT = mybir.ActivationFunctionType
MAX_ALL = bass.bass_isa.ReduceOp.max
ADD_ALL = bass.bass_isa.ReduceOp.add
AX = mybir.AxisListType

P = 128
GROUPS = 32
EPS = 1e-6


def attention_program(nc, x, gamma, beta, wq, bq, wk, wv, bv, wo, bo, out):
    B, C, H, W = x.shape
    N = H * W
    KC = C // P
    NJ = N // P
    HALF = N // 2
    CG = C // GROUPS
    SCALE = float(C) ** -0.5
    PIECES = N * KC // HALF
    BLOCK = 32
    assert HALF == 512 and C == 512 and NJ == 2 * KC and P % CG == 0 and B % 2 == 0 and B >= 4

    x_d = x.rearrange("b (k p) h w -> b p k (h w)", p=P)
    out_d = out.rearrange("b (k p) h w -> b k p (h w)", p=P)
    w_d = {n: a.rearrange("(k p) n -> p k n", p=P) for n, a in (("q", wq), ("k", wk), ("v", wv), ("o", wo))}
    bq_d, *vec_d = [a.rearrange("(k p) -> p k", p=P) for a in (bq, gamma, beta, bo)]

    with ExitStack() as ctx:
        def sb(name, shape, dt=F32):
            return ctx.enter_context(nc.sbuf_tensor(name, [P, *shape], dt))

        def sem(name):
            return ctx.enter_context(nc.semaphore(name))

        wkq_hi, wkq_lo = sb("wkq_hi", [KC, C], F32R), sb("wkq_lo", [KC, C], F32R)
        wov_hi, wov_lo = sb("wov_hi", [KC, C], F32R), sb("wov_lo", [KC, C], F32R)
        h_hi, h_lo = sb("h_hi", [KC, N], F32R), sb("h_lo", [KC, N], F32R)
        t_hi, t_lo = sb("t_hi", [KC, HALF], F32R), sb("t_lo", [KC, HALF], F32R)
        v_hi, v_lo = sb("v_hi", [NJ, C], F32R), sb("v_lo", [NJ, C], F32R)
        p_hi, p_lo = sb("p_hi", [NJ, HALF], F32R), sb("p_lo", [NJ, HALF], F32R)
        xt = sb("xt", [2, KC, N])
        scores = sb("scores", [NJ, HALF])
        stage = sb("stage", [2, HALF])
        run_max, all_max = sb("run_max", [HALF]), sb("all_max", [HALF])
        run_sum, inv_sum = sb("run_sum", [HALF]), sb("inv_sum", [HALF])
        ident = sb("ident", [P])
        bq_s, vecs = sb("bq_s", [KC]), sb("vecs", [3, KC])
        gamma_s, beta_s, bo_s = (vecs[:, n, :] for n in range(3))
        t_bias, out_bias, wo_bv = sb("t_bias", [KC]), sb("out_bias", [KC]), sb("wo_bv", [KC])
        bn = sb("bn", [PIECES, 6])
        chan, square = sb("chan", [BLOCK]), sb("square", [BLOCK])
        turned, sums, averages = sb("turned", [BLOCK]), sb("sums", [BLOCK // CG]), sb("averages", [BLOCK])
        chan_g, square_g, diff = sb("chan_g", [BLOCK]), sb("square_g", [BLOCK]), sb("diff", [KC])
        chan_kv, chan_g_kv = (a[:, 0:2 * KC].rearrange("p (k s) -> p k s", s=2) for a in (chan, chan_g))
        var_g, rstd, minus_half = sb("var_g", [KC]), sb("rstd", [KC]), sb("minus_half", [KC])
        h_scale, h_shift, mean_scaled = sb("h_scale", [KC]), sb("h_shift", [KC]), sb("mean_scaled", [KC])

        wq_raw, wk_raw = scores[:, 0:KC, :], scores[:, KC:2 * KC, :]
        raw = xt[:, 1, :, :].rearrange("p k n -> p (k n)")
        wv_raw = raw[:, 0:KC * C].rearrange("p (k n) -> p k n", k=KC)
        wo_raw = raw[:, KC * C:2 * KC * C].rearrange("p (k n) -> p k n", k=KC)
        wq_hi, wq_lo, wk_hi, wk_lo = v_hi[:, 0:KC, :], v_lo[:, 0:KC, :], v_hi[:, KC:NJ, :], v_lo[:, KC:NJ, :]
        wv_hi, wv_lo, wot_hi, wot_lo = p_hi[:, 0:KC, :], p_lo[:, 0:KC, :], p_hi[:, KC:NJ, :], p_lo[:, KC:NJ, :]
        bv_rows, wo_bv_terms = stage[:, 0, :], stage[:, 1, :]
        wk_bq_terms, t_bias_rows = run_max[:], all_max[:]

        bank = [ctx.enter_context(nc.psum_tensor(f"bank{n}", [P, 512], F32)) for n in range(8)]

        def t_bank(half, c):
            return bank[4 * half + c]

        def v_bank(j):
            return bank[(4 + j) % 8]

        def s_bank(half, j):
            return bank[j if half else (4 + j) % 8]

        def o_bank(half, c):
            return bank[4 * half + c]

        wv_in, wo_in, bq_in, vec_in, bv_in = (sem(n) for n in ("wv_in", "wo_in", "bq_in", "vec_in", "bv_in"))
        wk_in = [sem(f"wk_in{o}") for o in range(KC)]
        wq_in = [sem(f"wq_in{o}") for o in range(KC)]
        x0_in = [sem(f"x0_in{k}") for k in range(KC)]
        x_in = [sem("x_in0"), sem("x_in1")]
        out_stored = [sem("out_stored0"), sem("out_stored1")]
        consts_set, max_all, sum_all, rstd_set = (sem(n) for n in ("consts_set", "max_all", "sum_all", "rstd_set"))
        bq_summed = sem("bq_summed")
        reduce_begun = sem("reduce_begun")
        wkq_summed, wov_summed, wo_turned = (sem(n) for n in ("wkq_summed", "wov_summed", "wo_turned"))
        t_summed, v_summed, s_summed, o_summed = (sem(n) for n in ("t_summed", "v_summed", "s_summed", "o_summed"))
        p_used = sem("p_used")
        wk_high, wq_high, wv_high, wot_high, wkq_high, wov_high = (
            sem(n) for n in ("wk_high", "wq_high", "wv_high", "wot_high", "wkq_high", "wov_high"))
        t_high, v_high, h_high, p_high, s_copied, exp_set = (
            sem(n) for n in ("t_high", "v_high", "h_high", "p_high", "s_copied", "exp_set"))
        wk_split, wq_split, wv_split, wot_split, wkq_split, wov_split = (
            sem(n) for n in ("wk_split", "wq_split", "wv_split", "wot_split", "wkq_split", "wov_split"))
        bq_step, bv_used, diagonals_set, biases_set = (
            sem(n) for n in ("bq_step", "bv_used", "diagonals_set", "biases_set"))
        t_split, v_split, h_split, p_split = (sem(n) for n in ("t_split", "v_split", "h_split", "p_split"))
        max_step, centred, sum_step, inv_set = (sem(n) for n in ("max_step", "centred", "sum_step", "inv_set"))
        zeros_set, bn_set, chan_set, group_step, var_set, scale_step, h_full = (
            sem(n) for n in ("zeros_set", "bn_set", "chan_set", "group_step", "var_set", "scale_step", "h_full"))
        o_scaled, o_done = sem("o_scaled"), sem("o_done")

        block = ctx.enter_context(nc.Block())

        def images(engine, image):
            with engine.Fori(0, B - 2, 2) as b:
                image(b, 0, True)
                image(b + 1, 1, True)
            image(B - 2, 0, True)
            image(B - 1, 1, False)

        def count(b, per_image, step):
            return b * per_image + step

        @block.sync
        def _(sp):
            for o in range(KC):
                sp.dma_start(wk_raw[:, o, :], w_d["k"][:, o, :]).then_inc(wk_in[o], 16)
                sp.dma_start(wq_raw[:, o, :], w_d["q"][:, o, :]).then_inc(wq_in[o], 16)
            sp.dma_start(wo_raw, w_d["o"]).then_inc(wo_in, 16)
            sp.dma_start(wv_raw, w_d["v"]).then_inc(wv_in, 16)
            for k in range(KC):
                sp.dma_start(xt[:, 0, k, :], x_d[0][:, k, :]).then_inc(x0_in[k], 16)
            for s in range(2):
                sp.sem_inc(out_stored[s], 16)

            def image(b, par, more):
                if more:
                    sp.wait_ge(o_done, count(b, 8, 8))
                    sp.dma_start(xt[:, 1 - par, :, :], x_d[b + 1]).then_inc(x_in[1 - par], 16)
                for n in range(2 * KC):
                    half, c = divmod(n, KC)
                    sp.wait_ge(o_done, count(b, 8, 8 + n + 1))
                    sp.dma_start(out_d[b, c, :, half * HALF:(half + 1) * HALF],
                                 stage[:, n % 2, :]).then_inc(out_stored[n % 2], 16)

            images(sp, image)
            for s in range(2):
                sp.wait_ge(out_stored[s], 16 * (1 + B * KC))

        @block.gpsimd
        def _(pool):
            nc.gpsimd.memset(ident[:], 0.0).then_inc(consts_set, 1)
            nc.gpsimd.memset(minus_half[:], -0.5).then_inc(consts_set, 1)
            pool.wait_ge(consts_set, 2)
            nc.gpsimd.affine_select(out=ident[:], in_=ident[:], compare_op=ALU.not_equal, fill=1.0, base=0,
                                    pattern=[[-1, P]], channel_multiplier=1).then_inc(consts_set, 1)
            for o in range(KC):
                pool.wait_ge(wv_high, o + 1)
                nc.gpsimd.tensor_tensor(wv_lo[:, o, :], wv_raw[:, o, :], wv_hi[:, o, :].bitcast(F32),
                                        ALU.subtract).then_inc(wv_split, 1)

            pool.wait_ge(bq_step, KC)
            nc.gpsimd.partition_all_reduce(t_bias_rows, wk_bq_terms, P, ADD_ALL).then_inc(bq_summed, 1)

            def deviation(b):
                pool.wait_ge(var_set, count(b, 1, 1))
                nc.gpsimd.tensor_tensor(rstd[:], var_g[:], minus_half[:], ALU.pow).then_inc(rstd_set, 1)

            deviation(0)

            def image(b, par, more):
                for half in range(2):
                    pool.wait_ge(max_step, count(b, 2 * (NJ - 1), (half + 1) * (NJ - 1)))
                    pool.sem_inc(reduce_begun, 1)
                    nc.gpsimd.partition_all_reduce(all_max[:], run_max[:], P, MAX_ALL).then_inc(max_all, 1)
                    if half == 0 and more:
                        deviation(b + 1)
                    pool.wait_ge(sum_step, count(b, 2 * (NJ - 1), (half + 1) * (NJ - 1)))
                    pool.wait_ge(o_scaled, count(b, 8, 8 + half * KC))
                    pool.sem_inc(reduce_begun, 1)
                    nc.gpsimd.partition_all_reduce(inv_sum[:], run_sum[:], P, ADD_ALL).then_inc(sum_all, 1)

            images(pool, image)

        @block.tensor
        def _(pe):
            def product(o, a_hi, a_lo, b_hi, b_lo, start, stop):
                nc.tensor.matmul(o, a_hi, b_hi, start=start, stop=False)
                nc.tensor.matmul(o, a_hi, b_lo, start=False, stop=False)
                return nc.tensor.matmul(o, a_lo, b_hi, start=False, stop=stop)

            def cols(n):
                return slice(n * P, (n + 1) * P)

            for o in range(KC):
                pe.wait_ge(wk_split, o + 1)
                pe.wait_ge(wq_split, o + 1)
                for c in range(KC):
                    mm = product(bank[c][:], wq_hi[:, o, cols(c)], wq_lo[:, o, cols(c)],
                                 wk_hi[:, o, :], wk_lo[:, o, :], o == 0, o == KC - 1)
                    if o == KC - 1:
                        mm.then_inc(wkq_summed, 1)
                if o == KC - 2:
                    pe.wait_ge(wo_in, 16)
                    pe.wait_ge(consts_set, 3)
                    for n in range(KC):
                        for c in range(KC):
                            mm = nc.tensor.transpose(bank[4 + n][:, cols(c)], wo_raw[:, c, cols(n)], ident[:])
                        mm.then_inc(wo_turned, 1)
            for c in range(KC):
                pe.wait_ge(wot_split, KC)
                for o in range(KC):
                    pe.wait_ge(wv_split, o + 1)
                    mm = product(bank[4 + c][:], wv_hi[:, o, cols(c)], wv_lo[:, o, cols(c)],
                                 wot_hi[:, o, :], wot_lo[:, o, :], o == 0, o == KC - 1)
                mm.then_inc(wov_summed, 1)

            def t_part(half, c, k):
                q = slice(half * HALF, (half + 1) * HALF)
                return product(t_bank(half, c)[:], wkq_hi[:, k, cols(c)], wkq_lo[:, k, cols(c)],
                               h_hi[:, k, q], h_lo[:, k, q], k == 0, k == KC - 1)

            def make_t_0(b):
                for k in range(KC):
                    pe.wait_ge(h_split, count(b, PIECES, 2 * k + 1))
                    for c in range(KC):
                        if k == 0:
                            pe.wait_ge(o_scaled, count(b, 8, c + 1))
                        mm = t_part(0, c, k)
                        if k == KC - 1:
                            mm.then_inc(t_summed, 1)

            def make_t_1(b):
                for c in range(KC):
                    pe.wait_ge(s_copied, count(b, 16, c + 1))
                    for k in range(KC):
                        mm = t_part(1, c, k)
                    mm.then_inc(t_summed, 1)

            def make_v(b):
                for j in range(NJ):
                    if j < 4:
                        pe.wait_ge(o_scaled, count(b, 8, 4 + j + 1))
                    else:
                        pe.wait_ge(t_split, count(b, 8, j - 4 + 1))
                    if j == 4:
                        pe.wait_ge(h_split, count(b, PIECES, PIECES))
                    for k in range(KC):
                        if j == 0:
                            pe.wait_ge(wov_split, k + 1)
                        mm = product(v_bank(j)[:], h_hi[:, k, cols(j)], h_lo[:, k, cols(j)],
                                     wov_hi[:, k, :], wov_lo[:, k, :], k == 0, k == KC - 1)
                    mm.then_inc(v_summed, 1)

            def score(half, j, k):
                return product(s_bank(half, j)[:], h_hi[:, k, cols(j)], h_lo[:, k, cols(j)],
                               t_hi[:, k, :], t_lo[:, k, :], k == 0, k == KC - 1)

            def scores_0(b):
                pe.wait_ge(t_split, count(b, 8, KC))
                for j in range(NJ):
                    pe.wait_ge(v_split, count(b, 8, j + 1))
                    for k in range(KC):
                        mm = score(0, j, k)
                    mm.then_inc(s_summed, 1)

            def scores_1(b):
                for k in range(KC):
                    pe.wait_ge(t_split, count(b, 8, KC + k + 1))
                    for j in range(4):
                        if k == 0:
                            pe.wait_ge(s_copied, count(b, 16, j + 4 + 1))
                        mm = score(1, j, k)
                        if k == KC - 1:
                            mm.then_inc(s_summed, 1)
                for j in range(4, NJ):
                    for k in range(KC):
                        mm = score(1, j, k)
                    mm.then_inc(s_summed, 1)

            def last_outputs(b):
                for c in range(KC):
                    pe.wait_ge(s_copied, count(b, 16, NJ + 4 + c + 1))
                    for j in range(NJ):
                        if c == 0:
                            pe.wait_ge(p_split, count(b, 16, NJ + j + 1))
                        mm = product(o_bank(1, c)[:], v_hi[:, j, cols(c)], v_lo[:, j, cols(c)],
                                     p_hi[:, j, :], p_lo[:, j, :], j == 0, j == NJ - 1)
                    mm.then_inc(o_summed, 1)

            def outputs(b, half):
                for j in range(NJ):
                    pe.wait_ge(p_split, count(b, 16, half * NJ + j + 1))
                    for c in range(KC):
                        if j == 0:
                            pe.wait_ge(s_copied, count(b, 16, NJ + 4 * half + c + 1))
                        mm = product(o_bank(half, c)[:], v_hi[:, j, cols(c)], v_lo[:, j, cols(c)],
                                     p_hi[:, j, :], p_lo[:, j, :], j == 0, j == NJ - 1)
                        if j == NJ - 1:
                            mm.then_inc(o_summed, 1)
                    if half == 0 and j < NJ - 1:
                        mm.then_inc(p_used, 1)

            def image(b, par, more):
                make_t_0(b)
                make_v(b)
                scores_0(b)
                make_t_1(b)
                scores_1(b)
                pe.wait_ge(v_split, count(b, 8, NJ))
                outputs(b, 0)
                if more:
                    outputs(b, 1)
                else:
                    last_outputs(b)

            images(pe, image)

        @block.scalar
        def _(act):
            act.dma_start(bq_s[:], bq_d, allow_slow_non_contiguous=True).then_inc(bq_in, 16)
            nc.scalar.preload_act_table(ACT.Exp)
            for o in range(KC):
                act.wait_ge(wk_in[o], 16)
                nc.scalar.copy(wk_hi[:, o, :], wk_raw[:, o, :]).then_inc(wk_high, 1)
                act.wait_ge(wq_in[o], 16)
                nc.scalar.copy(wq_hi[:, o, :], wq_raw[:, o, :]).then_inc(wq_high, 1)
                if o == 1:
                    for n, a in enumerate(vec_d):
                        act.dma_start(vecs[:, n, :], a, allow_slow_non_contiguous=True).then_inc(vec_in, 16)
                    act.dma_start(bv_rows, bv.partition_broadcast(P)).then_inc(bv_in, 16)
            act.wait_ge(wv_in, 16)
            for o in range(KC):
                nc.scalar.copy(wv_hi[:, o, :], wv_raw[:, o, :]).then_inc(wv_high, 1)
            for o in range(KC):
                act.wait_ge(wo_turned, o + 1)
                nc.scalar.copy(wot_hi[:, o, :], bank[4 + o][:]).then_inc(wot_high, 1)
            for c in range(KC):
                act.wait_ge(wkq_summed, c + 1)
                nc.scalar.copy(wkq_hi[:, c, :], bank[c][:]).then_inc(wkq_high, 1)

            def high_h(b, par, k):
                act.wait_ge(scale_step, count(b, 3, 3))
                nc.scalar.activation(h_hi[:, k, :], xt[:, par, k, :], ACT.Identity, bias=h_shift[:, k:k + 1],
                                     scale=h_scale[:, k:k + 1]).then_inc(h_high, 1)

            for k in range(KC):
                high_h(0, 0, k)
            for c in range(KC):
                act.wait_ge(wov_summed, c + 1)
                nc.scalar.copy(wov_hi[:, c, :], bank[4 + c][:]).then_inc(wov_high, 1)

            act.wait_ge(diagonals_set, KC)

            def high_t(b, half, c):
                act.wait_ge(t_summed, count(b, 8, half * KC + c + 1))
                nc.scalar.activation(t_hi[:, c, :], t_bank(half, c)[:], ACT.Identity,
                                     bias=t_bias[:, c:c + 1]).then_inc(t_high, 1)

            def copy_scores(b, half, j):
                act.wait_ge(s_summed, count(b, 16, half * NJ + j + 1))
                if half == 0:
                    act.wait_ge(h_split, count(b, PIECES, j + 1))
                else:
                    act.wait_ge(sum_step, count(b, 2 * (NJ - 1), max(j, 1)))
                nc.scalar.copy(scores[:, j, :], s_bank(half, j)[:]).then_inc(s_copied, 1)

            def exponentials(b, half, j):
                act.wait_ge(centred, count(b, 16, half * NJ + j + 1))
                nc.scalar.activation(scores[:, j, :], scores[:, j, :], ACT.Exp, scale=SCALE).then_inc(exp_set, 1)

            def high_p(b, half, j):
                act.wait_ge(exp_set, count(b, 16, half * NJ + j + 1))
                if half == 1 and j < NJ - 1:
                    act.wait_ge(p_used, count(b, NJ - 1, j + 1))
                elif half == 1:
                    act.wait_ge(o_summed, count(b, 8, KC))
                nc.scalar.copy(p_hi[:, j, :], scores[:, j, :]).then_inc(p_high, 1)

            def image(b, par, more):
                for c in range(KC):
                    high_t(b, 0, c)
                for j in range(NJ):
                    act.wait_ge(v_summed, count(b, 8, j + 1))
                    nc.scalar.copy(v_hi[:, j, :], v_bank(j)[:]).then_inc(v_high, 1)
                for j in range(NJ):
                    copy_scores(b, 0, j)
                high_t(b, 1, 0)
                exponentials(b, 0, 0)
                for j in range(NJ):
                    if 1 <= j < KC:
                        high_t(b, 1, j)
                    if j + 1 < NJ:
                        exponentials(b, 0, j + 1)
                    high_p(b, 0, j)
                for j in range(NJ):
                    copy_scores(b, 1, j)
                exponentials(b, 1, 0)
                for j in range(NJ):
                    if j + 1 < NJ:
                        exponentials(b, 1, j + 1)
                    high_p(b, 1, j)
                    if more and j < KC:
                        high_h(b + 1, 1 - par, j)

            images(act, image)

        @block.vector
        def _(dve):
            def piece_of(par, n):
                k, half = divmod(n, 2)
                return k, xt[:, par, k, half * HALF:(half + 1) * HALF]

            def bn_piece(b, par, n):
                k, piece = piece_of(par, n)
                nc.vector.bn_stats(bn[:, n, :], piece).then_inc(bn_set, 1)

            def channel_stats(b):
                for k in range(KC):
                    nc.vector.bn_aggr(chan_kv[:, k, :],
                                       bn[:, 2 * k:2 * k + 2, :].rearrange("p a s -> p (a s)")).then_inc(chan_set, 1)

            def group_average(b, at, out, of):
                nc.vector.transpose(turned[:], of).then_inc(group_step, 1)
                dve.wait_ge(group_step, count(b, 10, at + 1))
                nc.vector.tensor_reduce(sums[:], turned[:].rearrange("p (g d) -> p g d", d=CG), AX.X,
                                        ALU.add).then_inc(group_step, 1)
                dve.wait_ge(group_step, count(b, 10, at + 2))
                nc.vector.tensor_scalar(averages[:].rearrange("p (g d) -> p g d", d=CG),
                                        sums[:].unsqueeze(2).to_broadcast([P, BLOCK // CG, CG]), 1.0 / CG, None,
                                        ALU.mult).then_inc(group_step, 1)
                dve.wait_ge(group_step, count(b, 10, at + 3))
                nc.vector.transpose(out, averages[:]).then_inc(group_step, 1)

            def group_variance(b):
                dve.wait_ge(chan_set, count(b, KC, KC))
                group_average(b, 0, chan_g[:], chan[:])
                dve.wait_ge(group_step, count(b, 10, 4))
                nc.vector.tensor_tensor(diff[:], chan_kv[:, :, 0], chan_g_kv[:, :, 0],
                                        ALU.subtract).then_inc(group_step, 1)
                dve.wait_ge(group_step, count(b, 10, 5))
                nc.vector.tensor_tensor(square[:, 0:KC], diff[:], diff[:], ALU.mult).then_inc(group_step, 1)
                dve.wait_ge(group_step, count(b, 10, 6))
                group_average(b, 6, square_g[:], square[:])
                dve.wait_ge(group_step, count(b, 10, 10))
                nc.vector.scalar_tensor_tensor(var_g[:], square_g[:, 0:KC], EPS, chan_g_kv[:, :, 1], ALU.add,
                                               ALU.add).then_inc(var_set, 1)

            def affine(b):
                dve.wait_ge(rstd_set, count(b, 1, 1))
                nc.vector.tensor_tensor(h_scale[:], gamma_s, rstd[:], ALU.mult).then_inc(scale_step, 1)
                dve.wait_ge(scale_step, count(b, 3, 1))
                nc.vector.tensor_tensor(mean_scaled[:], chan_g_kv[:, :, 0], h_scale[:],
                                        ALU.mult).then_inc(scale_step, 1)
                dve.wait_ge(scale_step, count(b, 3, 2))
                nc.vector.tensor_tensor(h_shift[:], beta_s, mean_scaled[:], ALU.subtract).then_inc(scale_step, 1)

            def low_h(b, par, n, slot):
                k, piece = piece_of(par, n)
                dve.wait_ge(scale_step, count(b, 3, 3))
                nc.vector.tensor_scalar(scores[:, slot, :], piece, h_scale[:, k:k + 1], h_shift[:, k:k + 1],
                                        ALU.mult, ALU.add).then_inc(h_full, 1)
                q = slice((n % 2) * HALF, (n % 2 + 1) * HALF)
                dve.wait_ge(h_full, count(b, PIECES, n + 1))
                dve.wait_ge(h_high, count(b, KC, k + 1))
                nc.vector.tensor_tensor(h_lo[:, k, q], scores[:, slot, :], h_hi[:, k, q].bitcast(F32),
                                        ALU.subtract).then_inc(h_split, 1)

            nc.vector.memset(chan[:], 0.0).then_inc(zeros_set, 1)
            nc.vector.memset(square[:], 0.0).then_inc(zeros_set, 1)
            for o in range(KC):
                dve.wait_ge(wk_high, o + 1)
                nc.vector.tensor_tensor(wk_lo[:, o, :], wk_raw[:, o, :], wk_hi[:, o, :].bitcast(F32),
                                        ALU.subtract).then_inc(wk_split, 1)
                dve.wait_ge(wq_high, o + 1)
                nc.vector.tensor_tensor(wq_lo[:, o, :], wq_raw[:, o, :], wq_hi[:, o, :].bitcast(F32),
                                        ALU.subtract).then_inc(wq_split, 1)
            dve.wait_ge(bq_in, 16)
            nc.vector.tensor_scalar(wk_bq_terms, wk_raw[:, 0, :], bq_s[:, 0:1], None, ALU.mult).then_inc(bq_step, 1)
            for o in range(1, KC):
                dve.wait_ge(bq_step, o)
                nc.vector.scalar_tensor_tensor(wk_bq_terms, wk_raw[:, o, :], bq_s[:, o:o + 1], wk_bq_terms,
                                               ALU.mult, ALU.add).then_inc(bq_step, 1)
            for n in range(PIECES):
                dve.wait_ge(x0_in[n // 2], 16)
                bn_piece(0, 0, n)
                if n == 1:
                    for o in range(KC):
                        dve.wait_ge(wot_high, o + 1)
                        nc.vector.tensor_tensor(wot_lo[:, o, :], bank[4 + o][:], wot_hi[:, o, :].bitcast(F32),
                                                ALU.subtract).then_inc(wot_split, 1)
            dve.wait_ge(zeros_set, 2)
            dve.wait_ge(bn_set, PIECES)
            channel_stats(0)
            dve.wait_ge(wkq_high, 1)
            nc.vector.tensor_tensor(wkq_lo[:, 0, :], bank[0][:], wkq_hi[:, 0, :].bitcast(F32),
                                    ALU.subtract).then_inc(wkq_split, 1)
            group_variance(0)
            for c in range(1, KC):
                if c == KC - 1:
                    dve.wait_ge(vec_in, 16 * len(vec_d))
                    affine(0)
                dve.wait_ge(wkq_high, c + 1)
                nc.vector.tensor_tensor(wkq_lo[:, c, :], bank[c][:], wkq_hi[:, c, :].bitcast(F32),
                                        ALU.subtract).then_inc(wkq_split, 1)
            dve.wait_ge(wkq_split, KC)
            dve.sem_inc(o_scaled, 4)
            for n in range(PIECES):
                low_h(0, 0, n, n)
            for c in range(KC):
                dve.wait_ge(wov_high, c + 1)
                nc.vector.tensor_tensor(wov_lo[:, c, :], bank[4 + c][:], wov_hi[:, c, :].bitcast(F32),
                                        ALU.subtract).then_inc(wov_split, 1)
            dve.wait_ge(wov_split, KC)
            dve.sem_inc(o_scaled, 4)
            dve.wait_ge(bq_summed, 1)
            dve.wait_ge(consts_set, 3)
            for c in range(KC):
                if c:
                    dve.wait_ge(diagonals_set, c)
                nc.vector.tensor_tensor_reduce(out=wk_bq_terms[:, 0:P], in0=t_bias_rows[:, c * P:(c + 1) * P],
                                               in1=ident[:], scale=1.0, scalar=0.0, op0=ALU.mult, op1=ALU.add,
                                               accum_out=t_bias[:, c:c + 1]).then_inc(diagonals_set, 1)
            dve.wait_ge(diagonals_set, KC)
            dve.wait_ge(bv_in, 16)
            for c in range(KC):
                if c:
                    dve.wait_ge(bv_used, c)
                nc.vector.tensor_tensor_reduce(out=wo_bv_terms, in0=wo_raw[:, c, :], in1=bv_rows, scale=1.0,
                                               scalar=0.0, op0=ALU.mult, op1=ALU.add,
                                               accum_out=wo_bv[:, c:c + 1]).then_inc(bv_used, 1)
            dve.wait_ge(bv_used, KC)
            nc.vector.tensor_tensor(out_bias[:], wo_bv[:], bo_s, ALU.add).then_inc(biases_set, 1)
            dve.wait_ge(biases_set, 1)
            dve.sem_inc(o_done, 8)

            def low_t(b, half, c):
                dve.wait_ge(t_high, count(b, 8, half * KC + c + 1))
                nc.vector.scalar_tensor_tensor(t_lo[:, c, :], t_bank(half, c)[:], t_bias[:, c:c + 1],
                                               t_hi[:, c, :].bitcast(F32), ALU.add, ALU.subtract).then_inc(t_split, 1)

            def maximum(b, half, j):
                dve.wait_ge(s_copied, count(b, 16, half * NJ + j + 1))
                if j >= 2:
                    dve.wait_ge(max_step, count(b, 2 * (NJ - 1), half * (NJ - 1) + j - 1))
                before = scores[:, 0, :] if j == 1 else run_max[:]
                nc.vector.tensor_tensor(run_max[:], before, scores[:, j, :], ALU.max).then_inc(max_step, 1)

            def centre(b, half, j):
                dve.wait_ge(max_all, count(b, 2, half + 1))
                nc.vector.tensor_tensor(scores[:, j, :], scores[:, j, :], all_max[:], ALU.subtract).then_inc(centred, 1)

            def low_p(b, half, j):
                dve.wait_ge(p_high, count(b, 16, half * NJ + j + 1))
                nc.vector.tensor_tensor(p_lo[:, j, :], scores[:, j, :], p_hi[:, j, :].bitcast(F32),
                                        ALU.subtract).then_inc(p_split, 1)

            def add_up(b, half, j):
                if j >= 2:
                    dve.wait_ge(sum_step, count(b, 2 * (NJ - 1), half * (NJ - 1) + j - 1))
                before = scores[:, 0, :] if j == 1 else run_sum[:]
                nc.vector.tensor_tensor(run_sum[:], before, scores[:, j, :], ALU.add).then_inc(sum_step, 1)

            def inverse(b, half):
                dve.wait_ge(sum_all, count(b, 2, half + 1))
                nc.vector.reciprocal(inv_sum[:], inv_sum[:]).then_inc(inv_set, 1)

            def scale_out(b, n):
                half, c = divmod(n, KC)
                dve.wait_ge(o_summed, count(b, 8, n + 1))
                dve.wait_ge(out_stored[n % 2], count(b, 16 * KC, 16 * (n // 2 + 1)))
                dve.wait_ge(inv_set, count(b, 2, half + 1))
                nc.vector.tensor_tensor(stage[:, n % 2, :], o_bank(half, c)[:], inv_sum[:],
                                        ALU.mult).then_inc(o_scaled, 1)

            def add_residual(b, par, n):
                half, c = divmod(n, KC)
                dve.wait_ge(o_scaled, count(b, 8, 8 + n + 1))
                nc.vector.scalar_tensor_tensor(stage[:, n % 2, :], xt[:, par, c, half * HALF:(half + 1) * HALF],
                                               out_bias[:, c:c + 1], stage[:, n % 2, :], ALU.add,
                                               ALU.add).then_inc(o_done, 1)

            def next_h(b, par, n):
                dve.wait_ge(sum_step, count(b, 2 * (NJ - 1), NJ - 1 + max(n, 1)))
                low_h(b + 1, 1 - par, n, n)

            def outputs(b, par, half):
                for n in range(half * KC, (half + 1) * KC, 2):
                    scale_out(b, n)
                    scale_out(b, n + 1)
                    add_residual(b, par, n)
                    add_residual(b, par, n + 1)

            def image(b, par, more):
                for c in range(KC):
                    low_t(b, 0, c)
                for j in range(NJ):
                    dve.wait_ge(v_high, count(b, 8, j + 1))
                    nc.vector.tensor_tensor(v_lo[:, j, :], v_bank(j)[:], v_hi[:, j, :].bitcast(F32),
                                            ALU.subtract).then_inc(v_split, 1)
                if more:
                    dve.wait_ge(x_in[1 - par], count(b, 8, 16 - 8 * par))
                for j in range(NJ):
                    if more:
                        bn_piece(b + 1, 1 - par, j)
                    if j >= 1:
                        if more and j == NJ - 1:
                            dve.wait_ge(bn_set, count(b, PIECES, 2 * PIECES))
                        maximum(b, 0, j)
                if more:
                    channel_stats(b + 1)
                    group_variance(b + 1)
                centre(b, 0, 0)
                centre(b, 0, 1)
                for j in range(NJ):
                    if 1 <= j <= KC:
                        low_t(b, 1, j - 1)
                    if j == 2 and more:
                        affine(b + 1)
                    if j + 2 < NJ:
                        centre(b, 0, j + 2)
                    low_p(b, 0, j)
                    if j >= 1:
                        add_up(b, 0, j)
                inverse(b, 0)
                for j in range(1, NJ):
                    maximum(b, 1, j)
                centre(b, 1, 0)
                centre(b, 1, 1)
                for j in range(NJ):
                    if j + 2 < NJ:
                        centre(b, 1, j + 2)
                    low_p(b, 1, j)
                    if j >= 1:
                        add_up(b, 1, j)
                    if more and j >= 2:
                        next_h(b, par, j - 2)
                if more:
                    next_h(b, par, NJ - 2)
                    next_h(b, par, NJ - 1)
                outputs(b, par, 0)
                inverse(b, 1)
                if more:
                    outputs(b, par, 1)
                else:
                    for n in range(KC, 2 * KC):
                        scale_out(b, n)
                        add_residual(b, par, n)

            images(dve, image)


_TAKEN = {"x": "x", "L0_conv_norm_gamma": "gamma", "L0_conv_norm_beta": "beta", "L0_conv_wq": "wq",
          "L0_conv_bq": "bq", "L0_conv_wk": "wk", "L0_conv_wv": "wv", "L0_conv_bv": "bv",
          "L0_conv_wo": "wo", "L0_conv_bo": "bo"}


def kernel(**inputs):
    import numpy as np
    import concourse.bacc as bacc
    from concourse.bass_utils import run_bass_kernel_spmd

    nc = bacc.Bacc("TRN2", target_bir_lowering=False, num_devices=1)
    arrays, args = {}, {}
    for name, short in _TAKEN.items():
        a = np.ascontiguousarray(inputs[name])
        arrays[f"in_{short}"] = a
        args[short] = nc.dram_tensor(f"in_{short}", a.shape, mybir.dt.from_np(a.dtype), kind="ExternalInput").ap()
    shape = arrays["in_x"].shape
    args["out"] = nc.dram_tensor("out", shape, F32, kind="ExternalOutput").ap()
    attention_program(nc, **args)
    r = run_bass_kernel_spmd(nc, [arrays], core_ids=[0])
    return r.results[0]["out"]
```
